# Optimizing a Trainium2 kernel written in Bass

```python
import numpy as np
import jax
import jax.numpy as jnp

def _softmax(x, axis=-1):
    return jax.nn.softmax(x, axis=axis)

def _gelu(x):
    return jax.nn.gelu(x, approximate=True)

def _silu(x):
    return jax.nn.silu(x)

def _sigmoid(x):
    return jax.nn.sigmoid(x)

def _layernorm(x, axis=-1, eps=1e-05):
    m = jnp.mean(x, axis=axis, keepdims=True)
    v = jnp.var(x, axis=axis, keepdims=True)
    return (x - m) / jnp.sqrt(v + eps)

def _scatter_add(tgt, idx, src, axis=0):
    return tgt.at[idx].add(src)

def _segment_sum(src, seg, n):
    return jax.ops.segment_sum(src, seg, n)
kernel_name = 'mk_gnn_preln_d2_gnn_r8_ad20fe'

def setup_inputs(seed: int=0):
    np.random.seed(seed)
    _w = jnp.asarray

    def _rec_inputs():
        import jax
        import jax.numpy as jnp
        _gk = jax.random.key(seed)
        x = -0.0005121 + 1.001 * jax.random.normal(jax.random.fold_in(_gk, 1), (12500, 32), jnp.float32)
        src = jax.random.randint(jax.random.fold_in(_gk, 2), (200000,), 0, 12500, jnp.int32)
        dst = jax.random.randint(jax.random.fold_in(_gk, 3), (200000,), 0, 12500, jnp.int32)
        _o = jnp.argsort(dst, stable=True)
        src = src[_o]
        dst = dst[_o]
        edge_attr_3 = 0.000549083 + 1.00031 * jax.random.normal(jax.random.fold_in(_gk, 12), (200000, 3), jnp.float32)
        edge_attr_5 = -0.000325185 + 1.00005 * jax.random.normal(jax.random.fold_in(_gk, 13), (200000, 5), jnp.float32)
        edge_type_86 = jax.random.randint(jax.random.fold_in(_gk, 15), (200000,), 0, 86, jnp.int32)
        edge_weight1 = 0.000452788 + 0.999756 * jax.random.normal(jax.random.fold_in(_gk, 16), (200000, 1), jnp.float32)
        return (x, src, dst, edge_attr_3, edge_attr_5, edge_type_86, edge_weight1)
    x, src, dst, edge_attr_3, edge_attr_5, edge_type_86, edge_weight1 = _rec_inputs()

    def _L0_gnn_setup():
        import jax, jax.numpy as jnp
        import numpy as np
        import math
        M = 8
        COMBOS = [(0, 0, 0), (0, 1, 1), (1, 0, 1), (1, 1, 0), (1, 1, 1), (2, 1, 1)]

        def _cg_coeff(j1, m1, j2, m2, j3, m3):
            if m3 != m1 + m2:
                return 0.0
            f = math.factorial
            vmin = max(0, j2 - j3 - m1, j1 + m2 - j3)
            vmax = min(j1 + j2 - j3, j1 - m1, j2 + m2)
            pref = (2 * j3 + 1) * f(j3 + j1 - j2) * f(j3 - j1 + j2) * f(j1 + j2 - j3) / f(j1 + j2 + j3 + 1)
            pref *= f(j3 + m3) * f(j3 - m3) * f(j1 - m1) * f(j1 + m1) * f(j2 - m2) * f(j2 + m2)
            s = 0.0
            for v in range(vmin, vmax + 1):
                s += (-1) ** v / (f(v) * f(j1 + j2 - j3 - v) * f(j1 - m1 - v) * f(j2 + m2 - v) * f(j3 - j2 + m1 + v) * f(j3 - j1 - m2 + v))
            return math.sqrt(pref) * s

        def _su2_cg(l1, l2, l3):
            C = np.zeros((2 * l1 + 1, 2 * l2 + 1, 2 * l3 + 1), dtype=np.complex128)
            for m1 in range(-l1, l1 + 1):
                for m2 in range(-l2, l2 + 1):
                    m3 = m1 + m2
                    if -l3 <= m3 <= l3:
                        C[m1 + l1, m2 + l2, m3 + l3] = _cg_coeff(l1, m1, l2, m2, l3, m3)
            return C

        def _qmat(l):
            q = np.zeros((2 * l + 1, 2 * l + 1), dtype=np.complex128)
            for m in range(-l, 0):
                q[l + m, l + abs(m)] = 1 / np.sqrt(2)
                q[l + m, l - abs(m)] = -1j / np.sqrt(2)
            q[l, l] = 1.0
            for m in range(1, l + 1):
                q[l + m, l + abs(m)] = (-1) ** m / np.sqrt(2)
                q[l + m, l - abs(m)] = 1j * (-1) ** m / np.sqrt(2)
            return (-1j) ** l * q

        def _so3_cg(l1, l2, l3):
            C = np.einsum('ij,kl,mn,ikn->jlm', _qmat(l1), _qmat(l2), np.conj(_qmat(l3)).T, _su2_cg(l1, l2, l3))
            assert np.abs(C.imag).max() < 1e-06
            C = C.real
            return C / np.linalg.norm(C)
        CG = {c: jnp.asarray(_so3_cg(*c), dtype=jnp.float32) for c in COMBOS}
        N, E = (12500, 200000)
        ks = jax.random.split(jax.random.key(seed), 6)
        return {'node_irreps': jax.random.normal(ks[0], (N, 4 * M), jnp.float32), 'edge_index': jax.random.randint(ks[1], (2, E), 0, N, dtype=jnp.int32), 'sh0': jax.random.normal(ks[2], (E, 1), jnp.float32), 'sh1': jax.random.normal(ks[3], (E, 3), jnp.float32), 'sh2': jax.random.normal(ks[4], (E, 5), jnp.float32), 'W': jax.random.normal(ks[5], (len(COMBOS), M, M), jnp.float32)}
    _L0_gnn_all = _L0_gnn_setup()
    _L0_gnn_in = {k: v for k, v in _L0_gnn_all.items() if k in ('W',)}
    del _L0_gnn_all

    def _L1_gnn_setup():
        import jax, jax.numpy as jnp
        import numpy as np
        N_NODES = 6250
        N_EDGES = 100000
        INP_DIM = 32
        OUT_DIM = 32
        ATTN_DIM = 32
        NUM_RELS = 86
        NUM_BASES = 16
        GAMMA = 0.0
        key = jax.random.key(seed)
        ks = jax.random.split(key, 12)
        return {'h': jax.random.normal(ks[0], (N_NODES, INP_DIM), jnp.float32), 'weight': jax.random.normal(ks[1], (NUM_BASES, INP_DIM, OUT_DIM), jnp.float32), 'w_comp': jax.random.normal(ks[2], (NUM_RELS, NUM_BASES), jnp.float32), 'self_loop_weight': jax.random.normal(ks[3], (INP_DIM, OUT_DIM), jnp.float32), 'A1_w': jax.random.normal(ks[4], (ATTN_DIM, INP_DIM), jnp.float32), 'A1_b': jax.random.normal(ks[5], (ATTN_DIM,), jnp.float32), 'A2_w': jax.random.normal(ks[6], (ATTN_DIM, INP_DIM), jnp.float32), 'A2_b': jax.random.normal(ks[7], (ATTN_DIM,), jnp.float32), 'rel_emb': jax.random.normal(ks[8], (NUM_RELS, ATTN_DIM), jnp.float32), 'src': jax.random.randint(ks[9], (N_EDGES,), 0, N_NODES, jnp.int32), 'dst': jax.random.randint(ks[10], (N_EDGES,), 0, N_NODES, jnp.int32), 'etype': jax.random.randint(ks[11], (N_EDGES,), 0, NUM_RELS, jnp.int32)}
    _L1_gnn_all = _L1_gnn_setup()
    _L1_gnn_in = {k: v for k, v in _L1_gnn_all.items() if k in ('weight', 'w_comp', 'self_loop_weight', 'A1_w', 'A1_b', 'A2_w', 'A2_b', 'rel_emb')}
    del _L1_gnn_all
    return {'x': x, 'src': src, 'dst': dst, 'edge_attr_3': edge_attr_3, 'edge_attr_5': edge_attr_5, 'edge_type_86': edge_type_86, 'edge_weight1': edge_weight1, 'L0_gnn_W': _L0_gnn_in['W'], 'L1_gnn_weight': _L1_gnn_in['weight'], 'L1_gnn_w_comp': _L1_gnn_in['w_comp'], 'L1_gnn_self_loop_weight': _L1_gnn_in['self_loop_weight'], 'L1_gnn_A1_w': _L1_gnn_in['A1_w'], 'L1_gnn_A1_b': _L1_gnn_in['A1_b'], 'L1_gnn_A2_w': _L1_gnn_in['A2_w'], 'L1_gnn_A2_b': _L1_gnn_in['A2_b'], 'L1_gnn_rel_emb': _L1_gnn_in['rel_emb']}

def reference(x, src, dst, edge_attr_3, edge_attr_5, edge_type_86, edge_weight1, L0_gnn_W, L1_gnn_weight, L1_gnn_w_comp, L1_gnn_self_loop_weight, L1_gnn_A1_w, L1_gnn_A1_b, L1_gnn_A2_w, L1_gnn_A2_b, L1_gnn_rel_emb):
    import jax
    import jax.numpy as jnp

    def _L0_gnn_ref(node_irreps, edge_index, sh0, sh1, sh2, W):
        import jax, jax.numpy as jnp
        import numpy as np
        import math
        M = 8
        COMBOS = [(0, 0, 0), (0, 1, 1), (1, 0, 1), (1, 1, 0), (1, 1, 1), (2, 1, 1)]

        def _cg_coeff(j1, m1, j2, m2, j3, m3):
            if m3 != m1 + m2:
                return 0.0
            f = math.factorial
            vmin = max(0, j2 - j3 - m1, j1 + m2 - j3)
            vmax = min(j1 + j2 - j3, j1 - m1, j2 + m2)
            pref = (2 * j3 + 1) * f(j3 + j1 - j2) * f(j3 - j1 + j2) * f(j1 + j2 - j3) / f(j1 + j2 + j3 + 1)
            pref *= f(j3 + m3) * f(j3 - m3) * f(j1 - m1) * f(j1 + m1) * f(j2 - m2) * f(j2 + m2)
            s = 0.0
            for v in range(vmin, vmax + 1):
                s += (-1) ** v / (f(v) * f(j1 + j2 - j3 - v) * f(j1 - m1 - v) * f(j2 + m2 - v) * f(j3 - j2 + m1 + v) * f(j3 - j1 - m2 + v))
            return math.sqrt(pref) * s

        def _su2_cg(l1, l2, l3):
            C = np.zeros((2 * l1 + 1, 2 * l2 + 1, 2 * l3 + 1), dtype=np.complex128)
            for m1 in range(-l1, l1 + 1):
                for m2 in range(-l2, l2 + 1):
                    m3 = m1 + m2
                    if -l3 <= m3 <= l3:
                        C[m1 + l1, m2 + l2, m3 + l3] = _cg_coeff(l1, m1, l2, m2, l3, m3)
            return C

        def _qmat(l):
            q = np.zeros((2 * l + 1, 2 * l + 1), dtype=np.complex128)
            for m in range(-l, 0):
                q[l + m, l + abs(m)] = 1 / np.sqrt(2)
                q[l + m, l - abs(m)] = -1j / np.sqrt(2)
            q[l, l] = 1.0
            for m in range(1, l + 1):
                q[l + m, l + abs(m)] = (-1) ** m / np.sqrt(2)
                q[l + m, l - abs(m)] = 1j * (-1) ** m / np.sqrt(2)
            return (-1j) ** l * q

        def _so3_cg(l1, l2, l3):
            C = np.einsum('ij,kl,mn,ikn->jlm', _qmat(l1), _qmat(l2), np.conj(_qmat(l3)).T, _su2_cg(l1, l2, l3))
            assert np.abs(C.imag).max() < 1e-06
            C = C.real
            return C / np.linalg.norm(C)
        CG = {c: jnp.asarray(_so3_cg(*c), dtype=jnp.float32) for c in COMBOS}
        N, E = (node_irreps.shape[0], edge_index.shape[1])
        src = node_irreps[edge_index[0]]
        feats = {0: src[:, :M][:, :, None], 1: src[:, M:].reshape(E, M, 3)}
        sh = {0: sh0, 1: sh1, 2: sh2}
        msg = {0: jnp.zeros((E, M, 1), node_irreps.dtype), 1: jnp.zeros((E, M, 3), node_irreps.dtype)}
        for idx, (le, ln, lo) in enumerate(COMBOS):
            base = jnp.einsum('ijk,ei,emj->emk', CG[le, ln, lo], sh[le], feats[ln])
            msg[lo] = msg[lo] + jnp.einsum('io,eik->eok', W[idx], base)
        tgt = edge_index[1]
        agg0 = jax.ops.segment_sum(msg[0].reshape(E, M), tgt, num_segments=N)
        agg1 = jax.ops.segment_sum(msg[1].reshape(E, 3 * M), tgt, num_segments=N)
        return jnp.concatenate([agg0, agg1], axis=1)

    def _L1_gnn_ref(h, weight, w_comp, self_loop_weight, A1_w, A1_b, A2_w, A2_b, rel_emb, src, dst, etype):
        import jax, jax.numpy as jnp
        import numpy as np
        N_NODES = 6250
        N_EDGES = 100000
        INP_DIM = 32
        OUT_DIM = 32
        ATTN_DIM = 32
        NUM_RELS = 86
        NUM_BASES = 16
        GAMMA = 0.0
        E = src.shape[0]
        N = h.shape[0]
        x = h[src]
        y = h[dst]
        c = w_comp[etype]
        xb = jnp.einsum('ei,bio->ebo', x, weight)
        msg = jnp.einsum('eb,ebo->eo', c, xb)
        x_hat = x @ A1_w.T + A1_b
        y_hat = y @ A2_w.T + A2_b + rel_emb[etype]
        scale = jnp.sqrt(jnp.asarray(INP_DIM, h.dtype))
        a = jnp.tanh(jax.nn.relu(jnp.sum(x_hat * y_hat, axis=-1) / scale))
        a = jnp.where(a > GAMMA, a, jnp.zeros_like(a))
        nei = jax.ops.segment_sum(a[:, None] * msg, dst, num_segments=N)
        last_e = jax.ops.segment_max(jnp.arange(E, dtype=jnp.int32), dst, num_segments=N)
        last_e = jnp.clip(last_e, 0, E - 1)
        curr = h[src[last_e]] @ self_loop_weight
        in_deg = jax.ops.segment_sum(jnp.ones((E,), h.dtype), dst, num_segments=N)
        h_new = jnp.where((in_deg > 0)[:, None], nei + curr, jnp.zeros_like(nei))
        return jax.nn.relu(h_new)
    edge_index = jnp.stack([src, dst])
    h = jnp.maximum(_layernorm(x, axis=-1), 0.0)
    x = x + _L0_gnn_ref(h, edge_index, edge_weight1, edge_attr_3, edge_attr_5, L0_gnn_W)
    h = jnp.maximum(_layernorm(x, axis=-1), 0.0)
    x = x + _L1_gnn_ref(h, L1_gnn_weight, L1_gnn_w_comp, L1_gnn_self_loop_weight, L1_gnn_A1_w, L1_gnn_A1_b, L1_gnn_A2_w, L1_gnn_A2_b, L1_gnn_rel_emb, src, dst, edge_type_86)
    return x

_drawn_inputs = setup_inputs


def setup_inputs(seed=0):
    import zlib

    import numpy as np

    out = dict(_drawn_inputs(seed))
    spreads = {}
    factors = {}
    for name, (base, spread) in spreads.items():
        noise = np.random.default_rng([zlib.crc32(name.encode()), seed]).standard_normal(out[name].shape)
        drawn = base * np.exp(spread * noise) if base else spread * noise
        out[name] = jnp.asarray(drawn.astype(out[name].dtype))
    for name, factor in factors.items():
        out[name] = (out[name] * factor).astype(out[name].dtype)
    return out
```

```python
import concourse.bass as bass
from concourse import mybir
from contextlib import ExitStack
import numpy as np

F32 = mybir.dt.float32
I32 = mybir.dt.int32
ALU = mybir.AluOpType
ACT = mybir.ActivationFunctionType
AX_X = mybir.AxisListType.X

N, F = 12500, 32
E = 200000
NREL, NBASE = 86, 16
P = 128
M = -(-N // P)
NPAD = M * P
NWIN = NPAD + P
J = 12
GE = P * J
FULL = E // GE
JT = -(-(E - FULL * GE) // P)
EPAD = FULL * GE + JT * P
NG = FULL + 1
NCH = 7
MC = M // NCH
KA = F + 1
KT = KA + NBASE
C0, C1 = 9, 17
PASSES = -(-N // P)
NOWHERE = 1 << 20
EPS = 1e-5
assert NCH * MC == M and FULL % 2 == 0 and JT < J


class Group:

    def __init__(self, i, r, k):
        self.i, self.r, self.k = i, r, k
        self.b = r % 2
        self.q = r % 4
        self.s = i * 4 + r
        self.tail = isinstance(self.s, int) and self.s == FULL
        self.nj = JT if self.tail else J

    def order(self):
        return self.k * NG + self.s + 1

    def order2(self):
        return self.k * len(range(self.b, NG, 2)) + self.i * 2 + self.r // 2 + 1

    def order4(self):
        return self.k * len(range(self.q, NG, 4)) + self.i + self.r // 4 + 1

    def gathers(self):
        a_pass = len(range(self.q, NG, 4)) * J
        if self.q == FULL % 4:
            a_pass -= J - JT
        if self.tail:
            return (self.k + 1) * a_pass
        return self.k * a_pass + self.i * J + (self.r // 4 + 1) * J


def wait(eng, sem, n):
    if not isinstance(n, int) or n > 0:
        eng.wait_ge(sem, n)


def over_steps(eng, k, body, lag):
    def step(i, r):
        body([Group(i, r - d, k) if not isinstance(i, int) or 0 <= i * 4 + r - d < NG else None for d in range(lag + 1)])
    for t in range(4):
        step(0, t)
    with eng.Fori(0, FULL // 4 - 1) as i:
        for u in range(4):
            step(i, 4 + u)
    for t in range(FULL // 4 * 4, NG + lag):
        step(0, t)


def build(nc, x, src, dst, etype, edge, ramp, cg, w0, w1, a1b, a2, a2b, relT, wcomp, out):
    h_table = [nc.dram_tensor(f"h_table{n}", (NPAD, F), F32).ap() for n in range(2)]
    p_table = nc.dram_tensor("p_table", (NWIN, KA), F32).ap()

    with ExitStack() as ctx:
        def sb(name, shape, dt=F32):
            return ctx.enter_context(nc.sbuf_tensor(name, shape, dt))

        def sem(name):
            return ctx.enter_context(nc.semaphore(name))

        ps = ctx.enter_context(nc.psum_tensor("ps", [P, 8, 512], F32))
        G_ps = [ps[:, 2 * b:2 * b + 2, :] for b in range(2)]
        ex_ps = ps[:, 4:6, :]
        gt_ps = ps[:, 6:8, :]
        outT_ps = [ps[0:F, 2 * b + 1, 256:384] for b in range(2)]
        agg_ps = [ps[:, b, 0:MC * F].rearrange("p (m f) -> p m f", f=F) for b in range(2)]
        hT_ps = ps[0:F, 2:6, :].rearrange("p b n -> p (b n)")
        p_ps = [ps[:, 6 + b, 0:MC * KA] for b in range(2)]

        ramp_sb = sb("ramp_sb", [P, P + 1])
        iota_row, iota_col = ramp_sb[:, 0:P], ramp_sb[:, P:P + 1]
        ident = sb("ident", [P, P])
        zero = sb("zero", [P, KA])
        eps = sb("eps", [P, 1])
        cg_sb = sb("cg_sb", [P, 3, F])
        w0_sb = sb("w0_sb", [P, 3, F])
        w0c = sb("w0c", [P, 3, F])
        w1_sb = sb("w1_sb", [P, 5, F])
        a1b_sb = sb("a1b_sb", [F, KA])
        a2_sb = sb("a2_sb", [F, F])
        a2b_sb = sb("a2b_sb", [F, 1])
        relT_sb = sb("relT_sb", [F, NREL])
        relb_sb = sb("relb_sb", [F, NREL])
        p_w = sb("p_w", [F, KA])
        rel_tab = sb("rel_tab", [NREL, KT])

        X = sb("X", [P, M, F])
        H = sb("H", [P, 2, MC, F])
        centred = sb("centred", [P, MC, F])
        squares = sb("squares", [P, MC, F])
        row_sum = sb("row_sum", [P, MC])
        row_var = sb("row_var", [P, MC])
        row_std = sb("row_std", [P, MC])
        row_rstd = sb("row_rstd", [P, MC])
        hT = sb("hT", [F, MC * P])
        p_rows = sb("p_rows", [P, 2, MC * KA])
        aggT = sb("aggT", [F, NWIN])

        bases = sb("bases", [1, 2, NG], I32)
        last_row = sb("last_row", [1, NG], I32)
        span = sb("span", [1, NG])
        span_max = sb("span_max", [1, 1])
        beyond = sb("beyond", [1, 1], I32)
        moved = sb("moved", [P, 2])

        idx = sb("idx", [P, 2, J], I32)
        dcol = sb("dcol", [P, 2, J], I32)
        dnext = sb("dnext", [P, 2, J], I32)
        bcol = sb("bcol", [P, 2, 1], I32)
        coef0 = sb("coef0", [P, 2, J, C0])
        dst_b = sb("dst_b", [P, 2, GE], I32)
        typ_b = sb("typ_b", [NREL, 2, GE], I32)
        p_win = sb("p_win", [P, 2, KA])
        xg = sb("xg", [P, 4, J, F])
        node0 = sb("node0", [P, 1])
        node_p = sb("node_p", [P, 1])
        rel = sb("rel", [P, J])
        S = sb("S", [P, 2, J, P])
        ST = sb("ST", [P, J, P])
        typT = sb("typT", [NREL, J, P])
        prod = sb("prod", [P, J, F])
        dots = sb("dots", [P, J])
        score = sb("score", [P, J])
        score_r = sb("score_r", [P, J])
        att = sb("att", [P, J])
        coef1 = sb("coef1", [P, 2, J, C1])
        msg = sb("msg", [P, 2, J, C1 * F])
        G_sb = sb("G_sb", [P, 5 * P])
        GT_sb = sb("GT_sb", [P, 5 * P])

        consts_in, weights_in, x_in, rows_in = sem("consts_in"), sem("weights_in"), sem("x_in"), sem("rows_in")
        out_done, pad_done = sem("out_done"), sem("pad_done")
        pad_zero, eps_set = sem("pad_zero"), sem("eps_set")
        ident_set, w0_set, relb_set = sem("ident_set"), sem("w0_set"), sem("relb_set")
        span_set, span_max_set, beyond_set = sem("span_set"), sem("span_max_set"), sem("beyond_set")
        pw_ps_ready, pw_set = sem("pw_ps_ready"), sem("pw_set")
        moved_zero = sem("moved_zero")
        sum_set, centred_set, squares_set, var_set = sem("sum_set"), sem("centred_set"), sem("squares_set"), sem("var_set")
        std_set, rstd_set, h_set = sem("std_set"), sem("rstd_set"), sem("h_set")
        h_stored = [[sem(f"h_stored{n}_{b}") for b in range(2)] for n in range(2)]
        agg_turned, sums_done, out_set = sem("agg_turned"), sem("sums_done"), sem("out_set")
        agg_used = sem("agg_used")
        agg_cleared = [sem("agg_cleared0"), sem("agg_cleared1")]
        h_turned, hT_set, p_mm, p_set = sem("h_turned"), sem("hT_set"), sem("p_mm"), sem("p_set")
        p_stored = [sem(f"p_stored{b}") for b in range(2)]

        class Edge:

            def __init__(self, n):
                self.idx_in = [sem(f"idx_in{n}_{b}") for b in range(2)]
                self.cols_in = [sem(f"cols_in{n}_{b}") for b in range(2)]
                self.coef_in = [sem(f"coef_in{n}_{b}") for b in range(2)]
                self.rows_in = [sem(f"bcast_in{n}_{b}") for b in range(2)]
                self.pwin_in = [sem(f"pwin_in{n}_{b}") for b in range(2)]
                self.gathered = [sem(f"gathered{n}_{q}") for q in range(4)]
                self.gather_go = sem(f"gather_go{n}")
                self.node0_set = sem(f"node0_set{n}")
                self.node_p_set = sem(f"node_p_set{n}")
                self.rel_set = sem(f"rel_set{n}")
                self.last_set = sem(f"last_set{n}")
                self.S_set = sem(f"S_set{n}")
                self.prepared = sem(f"prepared{n}")
                self.ex_done = sem(f"ex_done{n}")
                self.prod_set = sem(f"prod_set{n}")
                self.dots_set = sem(f"dots_set{n}")
                self.score_set = sem(f"score_set{n}")
                self.score_r_set = sem(f"score_r_set{n}")
                self.att_set = sem(f"att_set{n}")
                self.coef_set = sem(f"coef_set{n}")
                self.msg_set = sem(f"msg_set{n}")
                self.summed = sem(f"summed{n}")
                self.G_set = sem(f"G_set{n}")
                self.turned = sem(f"turned{n}")
                self.GT_set = sem(f"GT_set{n}")
                self.projected = sem(f"projected{n}")
                self.added = sem(f"added{n}")
                self.moved_on = sem(f"moved_on{n}")
                self.base_moved = sem(f"base_moved{n}")
                self.load_go = sem(f"load_go{n}")

        layers = [Edge(0), Edge(1)]
        block = ctx.enter_context(nc.Block())

        def all_passes(eng, passes):
            passes(0)
            eng.wait_ge(beyond_set, 1)
            more = eng.value_load(beyond[0:1, 0:1], min_val=0, max_val=1)
            with eng.If(more):
                with eng.Fori(1, PASSES) as k:
                    passes(k)

        @block.sync
        def _(sp):
            sp.dma_start(X[:], x.rearrange("(p m) f -> p m f", m=M)).then_inc(x_in, 16)
            sp.dma_start(ramp_sb[:], ramp).then_inc(consts_in, 16)
            with nc.allow_non_contiguous_dma(reason="one element of each group"):
                full = dst[0:FULL * GE].rearrange("(a g e) -> a g e", a=1, e=GE)
                for n in range(2):
                    sp.dma_start(bases[:, n, 0:FULL], full[:, :, 0]).then_inc(rows_in, 16)
                sp.dma_start(last_row[:, 0:FULL], full[:, :, GE - 1]).then_inc(rows_in, 16)
            one = dst.rearrange("(a e) -> a e", a=1)
            for n in range(2):
                sp.dma_start(bases[:, n, FULL:NG], one[:, FULL * GE:FULL * GE + 1]).then_inc(rows_in, 16)
            sp.dma_start(last_row[:, FULL:NG], one[:, E - 1:E]).then_inc(rows_in, 16)
            sp.dma_start(cg_sb[:], cg.rearrange("(c p) o -> p c o", p=P)).then_inc(weights_in, 16)
            sp.dma_start(w0_sb[:], w0.rearrange("(c p) o -> p c o", p=P)).then_inc(weights_in, 16)
            sp.dma_start(w1_sb[:], w1.rearrange("(c p) o -> p c o", p=P)).then_inc(weights_in, 16)
            sp.dma_start(a1b_sb[:], a1b).then_inc(weights_in, 16)
            sp.dma_start(a2_sb[:], a2).then_inc(weights_in, 16)
            sp.dma_start(a2b_sb[:], a2b).then_inc(weights_in, 16)
            sp.dma_start(relT_sb[:], relT).then_inc(weights_in, 16)
            sp.dma_start(rel_tab[:, KA:KT], wcomp).then_inc(weights_in, 16)
            sp.wait_ge(pad_zero, 1)
            sp.dma_start(p_table[NPAD:NWIN, :], zero[:]).then_inc(pad_done, 16)

            def store_h(n, c):
                table = h_table[n].rearrange("(p m) f -> p m f", m=M)
                sp.wait_ge(h_set, n * NCH + c + 1)
                sp.dma_start(table[:, c * MC:(c + 1) * MC, :], H[:, c % 2]).then_inc(h_stored[n][c % 2], 16)

            def store_p(c):
                table = p_table[0:NPAD, :].rearrange("(p m) k -> p m k", m=M)
                sp.wait_ge(p_set, c + 1)
                sp.dma_start(table[:, c * MC:(c + 1) * MC, :],
                             p_rows[:, c % 2].rearrange("p (m k) -> p m k", k=KA)).then_inc(p_stored[c % 2], 16)

            def edge_loads(n):
                L = layers[n]

                def of(v, g, off=0):
                    if g.tail:
                        return v[FULL * GE + off:EPAD + off].rearrange("(j p) -> p j", p=P)
                    return v[bass.ds(g.s * GE + off, GE)].rearrange("(p j) -> p j", j=J)

                def loads(g):
                    b, nj = g.b, g.nj
                    if isinstance(g.s, int) and g.s < 2:
                        if not isinstance(g.k, int):
                            sp.wait_ge(L.added, g.k * NG)
                            sp.wait_ge(L.base_moved, g.k)
                            sp.nop().then_inc(L.load_go, 1)
                    else:
                        back = Group(g.i, g.r - 2, g.k)
                        sp.wait_ge(L.gathered[back.q], back.gathers() * 16)
                        if n == 1:
                            sp.nop().then_inc(L.load_go, 1)
                    if n == 1:
                        base = sp.value_load(bases[0:1, n, bass.ds(g.s, 1)], min_val=0, max_val=NPAD)
                    with nc.allow_non_contiguous_dma(reason="last group, 128 edges a column"):
                        sp.dma_start(idx[:, b, 0:nj], of(src, g)).then_inc(L.idx_in[b], 16)
                        wait(sp, (L.prepared if n else L.S_set), g.order() - 2)
                        sp.dma_start(dcol[:, b, 0:nj], of(dst, g)).then_inc(L.cols_in[b], 16)
                        first = dst[FULL * GE:FULL * GE + 1] if g.tail else dst[bass.ds(g.s * GE, 1)]
                        sp.dma_start(bcol[:, b, :], first.partition_broadcast(P)).then_inc(L.cols_in[b], 16)
                        if n == 1:
                            sp.dma_start(dnext[:, b, 0:nj], of(dst, g, 1)).then_inc(L.cols_in[b], 16)
                            for v, to, np_ in ((dst, dst_b, P), (etype, typ_b, NREL)):
                                row = v[FULL * GE:EPAD] if g.tail else v[bass.ds(g.s * GE, GE)]
                                sp.dma_start(to[:, b, 0:nj * P], row.partition_broadcast(np_)).then_inc(L.rows_in[b], 16)
                            wait(sp, L.ex_done, g.order() - 2)
                            sp.dma_start(p_win[:, b, :], p_table[bass.ds(base, P), :]).then_inc(L.pwin_in[b], 16)
                    if n == 0:
                        wait(sp, L.msg_set, g.order() - 2)
                        if g.tail:
                            rows = edge[FULL * GE:EPAD, :].rearrange("(j p) c -> p j c", p=P)
                        else:
                            rows = edge[bass.ds(g.s * GE, GE), :].rearrange("(p j) c -> p j c", j=J)
                        sp.dma_start(coef0[:, b, 0:nj, :], rows).then_inc(L.coef_in[b], 16)

                all_passes(sp, lambda k: over_steps(sp, k, lambda gs: loads(gs[0]), 0))

            for c in range(NCH):
                store_h(0, c)
            sp.wait_ge(rows_in, 16 * 6)
            edge_loads(0)
            for b in range(2):
                sp.wait_ge(h_stored[0][b], 16 * len(range(b, NCH, 2)))
            for c in range(NCH + 1):
                if c < NCH:
                    store_h(1, c)
                if c >= 1:
                    store_p(c - 1)
            for b in range(2):
                sp.wait_ge(p_stored[b], 16 * len(range(b, NCH, 2)))
            sp.wait_ge(pad_done, 16)
            edge_loads(1)
            left = N - (P - 1) * M
            rows = out[0:(P - 1) * M, :].rearrange("(p m) f -> p m f", m=M)
            rest = out[(P - 1) * M:N, :].rearrange("(a m) f -> a m f", a=1)
            stores = 0
            for c in range(NCH):
                lo, hi = c * MC, (c + 1) * MC
                sp.wait_ge(out_set, c + 1)
                sp.dma_start(rows[0:112, lo:hi, :], X[0:112, lo:hi, :]).then_inc(out_done, 16)
                sp.dma_start(rows[112:P - 1, lo:hi, :], X[112:P - 1, lo:hi, :]).then_inc(out_done, 16)
                stores += 2
                if lo < left:
                    sp.dma_start(rest[:, lo:min(hi, left), :], X[P - 1:P, lo:min(hi, left), :]).then_inc(out_done, 16)
                    stores += 1
            sp.wait_ge(out_done, 16 * stores)

        @block.gpsimd
        def _(pool):
            def edge_gathers(n):
                L = layers[n]

                def gather(g):
                    pool.wait_ge(L.idx_in[g.b], g.order2() * 16)
                    pool.nop().then_inc(L.gather_go, 1)
                    wait(pool, L.msg_set, g.order() - 4)
                    pool.nop().then_inc(L.gather_go, 1)
                    for j in range(g.nj):
                        pool.indirect_dma_start(
                            xg[:, g.q, j, :], None, h_table[n],
                            bass.IndirectOffsetOnAxis(ap=idx[:, g.b, j:j + 1], axis=0)).then_inc(L.gathered[g.q], 16)

                all_passes(pool, lambda k: over_steps(pool, k, lambda gs: gather(gs[0]), 0))

            pool.memset(aggT[:], 0.0).then_inc(agg_cleared[0], 1)
            for b in range(2):
                pool.wait_ge(h_stored[0][b], 16 * len(range(b, NCH, 2)))
            edge_gathers(0)
            pool.wait_ge(agg_turned, NCH)
            pool.memset(aggT[:], 0.0).then_inc(agg_cleared[1], 1)
            for b in range(2):
                pool.wait_ge(h_stored[1][b], 16 * len(range(b, NCH, 2)))
            edge_gathers(1)

        @block.tensor
        def _(pe):
            def turn_agg(n, c):
                wait(pe, out_set if n else agg_used, c - 1)
                for m in range(MC):
                    at = c * MC + m
                    last = pe.transpose(agg_ps[c % 2][:, m, :], aggT[:, at:at + M * (P - 1) + 1:M], ident[0:F, 0:F])
                last.then_inc(agg_turned, 1)

            def node_tables(c):
                pe.wait_ge(h_set, NCH + c + 1)
                wait(pe, hT_set, c)
                for m in range(MC):
                    last = pe.transpose(hT_ps[:, m * P:(m + 1) * P], H[:, c % 2, m, :], ident[:])
                last.then_inc(h_turned, 1)
                pe.wait_ge(hT_set, c + 1)
                wait(pe, p_set, c - 1)
                for m in range(MC):
                    last = pe.matmul(p_ps[c % 2][:, m * KA:(m + 1) * KA], hT[:, m * P:(m + 1) * P], p_w[:],
                                     start=True, stop=True)
                last.then_inc(p_mm, 1)

            def edge_sums(n):
                L = layers[n]
                banks = [(0, C0)] if n == 0 else [(0, C0), (C0, C1)]
                width = (C0 if n == 0 else C1) * F
                weights = w0c if n == 0 else w1_sb
                chunks = [(o, min(P, width - o)) for o in range(0, width, P)]

                def attention_rows(g):
                    pe.wait_ge(L.prepared, g.order())
                    pe.wait_ge(L.pwin_in[g.b], g.order2() * 16)
                    wait(pe, L.coef_set, g.order() - 1)
                    for j in range(g.nj):
                        to = ex_ps[:, j // 6, j % 6 * KT:j % 6 * KT + KT]
                        pe.matmul(to, typT[:, j, :], rel_tab[:], start=True, stop=False)
                        last = pe.matmul(to[:, 0:KA], ST[:, j, :], p_win[:, g.b, :], start=False, stop=True)
                    last.then_inc(L.ex_done, 1)

                def sum_edges(g, back):
                    wait(pe, L.G_set, g.order() - 2)
                    wait(pe, L.added, g.order() - 2)
                    pe.wait_ge(L.S_set, g.order())
                    pe.wait_ge(L.msg_set, g.order())
                    for j in range(g.nj):
                        for at, (lo, hi) in enumerate(banks):
                            last = pe.matmul(G_ps[g.b][:, at, 0:(hi - lo) * F], S[:, g.b, j, :],
                                             msg[:, g.b, j, lo * F:hi * F], start=(j == 0), stop=(j == g.nj - 1))
                        if j == g.nj - 1:
                            last.then_inc(L.summed, 1)
                        if j == min(g.nj, J // 3) - 1 and back:
                            project(back)

                def turn(g):
                    pe.wait_ge(L.G_set, g.order())
                    wait(pe, L.GT_set, g.order() - 1)
                    for c, (o, w) in enumerate(chunks):
                        last = pe.transpose(gt_ps[0:w, c // 4, c % 4 * P:c % 4 * P + P], G_sb[:, o:o + w], ident[:])
                    last.then_inc(L.turned, 1)

                def project(g):
                    pe.wait_ge(L.GT_set, g.order())
                    for c, (o, w) in enumerate(chunks):
                        last = pe.matmul(outT_ps[g.b], weights[0:w, c, :], GT_sb[0:w, c * P:(c + 1) * P],
                                         start=(c == 0), stop=(c == len(chunks) - 1))
                    last.then_inc(L.projected, 1)

                def step(gs):
                    if n == 1 and gs[0]:
                        attention_rows(gs[0])
                    if gs[2]:
                        turn(gs[2])
                    if gs[1]:
                        sum_edges(gs[1], gs[2])
                    elif gs[2]:
                        project(gs[2])

                all_passes(pe, lambda k: over_steps(pe, k, step, 2))

            pe.wait_ge(weights_in, 128)
            pe.wait_ge(relb_set, 1)
            pe.matmul(ps[0:F, 6, 0:KA], a2_sb[:], a1b_sb[:], start=True, stop=True)
            pe.matmul(ps[0:NREL, 7, 0:KA], relb_sb[:], a1b_sb[:], start=True, stop=True).then_inc(pw_ps_ready, 1)
            pe.wait_ge(ident_set, 1)
            pe.wait_ge(w0_set, 1)
            pe.wait_ge(pw_set, 2)
            edge_sums(0)
            pe.wait_ge(sums_done, 1)
            for c in range(NCH + 1):
                if c < NCH:
                    turn_agg(0, c)
                if c >= 1:
                    node_tables(c - 1)
            pe.wait_ge(p_set, NCH)
            edge_sums(1)
            pe.wait_ge(sums_done, 2)
            for c in range(NCH):
                turn_agg(1, c)

        @block.scalar
        def _(act):
            def std(n):
                for c in range(NCH):
                    act.wait_ge(var_set, n * NCH + c + 1)
                    act.activation(row_std[:], row_var[:], ACT.Sqrt, bias=eps[:, 0:1], scale=1.0 / F).then_inc(std_set, 1)
                    if n == 1:
                        act.wait_ge(h_turned, c + 1)
                        wait(act, p_mm, c)
                        act.activation(hT[:], hT_ps[:, 0:MC * P], ACT.Copy).then_inc(hT_set, 1)
                        act.wait_ge(p_mm, c + 1)
                        if c >= 2:
                            act.wait_ge(p_stored[c % 2], 16 * (c // 2))
                        act.activation(p_rows[:, c % 2], p_ps[c % 2], ACT.Copy).then_inc(p_set, 1)

            def edge_copies(n):
                L = layers[n]
                widths = [C0 * F] if n == 0 else [C0 * F, (C1 - C0) * F]

                def attention(g):
                    act.wait_ge(L.score_set, g.order())
                    act.activation(score_r[:, 0:g.nj], score[:, 0:g.nj], ACT.Relu).then_inc(L.score_r_set, 1)
                    act.wait_ge(L.score_r_set, g.order())
                    act.activation(att[:, 0:g.nj], score_r[:, 0:g.nj], ACT.Tanh, scale=float(F) ** -0.5)\
                       .then_inc(L.att_set, 1)

                def copy_G(g):
                    act.wait_ge(L.summed, g.order())
                    wait(act, L.turned, g.order() - 1)
                    at = 0
                    for b, w in enumerate(widths):
                        last = act.activation(G_sb[:, at:at + w], G_ps[g.b][:, b, 0:w], ACT.Copy)
                        at += w
                    last.then_inc(L.G_set, 1)

                def copy_GT(g):
                    act.wait_ge(L.turned, g.order())
                    wait(act, L.projected, g.order() - 1)
                    if n == 1:
                        act.activation(GT_sb[:, 0:4 * P], gt_ps[:, 0, :], ACT.Copy)
                        act.activation(GT_sb[0:F, 4 * P:5 * P], gt_ps[0:F, 1, 0:P], ACT.Copy).then_inc(L.GT_set, 1)
                    else:
                        act.activation(GT_sb[:, 0:2 * P], gt_ps[:, 0, 0:2 * P], ACT.Copy)
                        act.activation(GT_sb[0:F, 2 * P:3 * P], gt_ps[0:F, 0, 2 * P:3 * P], ACT.Copy).then_inc(L.GT_set, 1)

                def step(gs):
                    if n == 1 and gs[1]:
                        attention(gs[1])
                    if gs[2]:
                        copy_G(gs[2])
                        copy_GT(gs[2])

                all_passes(act, lambda k: over_steps(act, k, step, 2))

            act.wait_ge(eps_set, 1)
            std(0)
            act.wait_ge(pw_ps_ready, 1)
            act.activation(p_w[:], ps[0:F, 6, 0:KA], ACT.Copy).then_inc(pw_set, 1)
            act.activation(rel_tab[:, 0:KA], ps[0:NREL, 7, 0:KA], ACT.Copy).then_inc(pw_set, 1)
            edge_copies(0)
            std(1)
            edge_copies(1)

        @block.vector
        def _(dve):
            def layernorm(n, c):
                o = n * NCH + c + 1
                xc = X[:, c * MC:(c + 1) * MC, :]
                dve.tensor_reduce(row_sum[:], xc, AX_X, ALU.add).then_inc(sum_set, 1)
                dve.wait_ge(sum_set, o)
                dve.scalar_tensor_tensor(out=centred[:], in0=row_sum[:].unsqueeze(2).broadcast_to([P, MC, F]), scalar=-1.0 / F,
                                         in1=xc, op0=ALU.mult, op1=ALU.add).then_inc(centred_set, 1)
                dve.wait_ge(centred_set, o)
                dve.tensor_tensor(squares[:], centred[:], centred[:], ALU.mult).then_inc(squares_set, 1)
                dve.wait_ge(squares_set, o)
                dve.tensor_reduce(row_var[:], squares[:], AX_X, ALU.add).then_inc(var_set, 1)
                dve.wait_ge(std_set, o)
                dve.reciprocal(row_rstd[:], row_std[:]).then_inc(rstd_set, 1)
                dve.wait_ge(rstd_set, o)
                if c >= 2:
                    dve.wait_ge(h_stored[n][c % 2], 16 * (c // 2))
                    if n == 1:
                        dve.wait_ge(h_turned, c - 1)
                dve.scalar_tensor_tensor(out=H[:, c % 2], in0=centred[:], scalar=0.0,
                                         in1=row_rstd[:].unsqueeze(2).broadcast_to([P, MC, F]),
                                         op0=ALU.max, op1=ALU.mult).then_inc(h_set, 1)

            def edge_work(n):
                L = layers[n]
                C = C0 if n == 0 else C1
                ncols = 2 if n == 0 else 3

                def prepare(g):
                    b, nj, o = g.b, g.nj, g.order()
                    dve.wait_ge(L.cols_in[b], g.order2() * (16 * ncols))
                    dve.tensor_tensor(node0[:], bcol[:, b, :], moved[:, n:n + 1], ALU.add).then_inc(L.node0_set, 1)
                    dve.wait_ge(L.node0_set, o)
                    if n == 1:
                        dve.tensor_tensor(node_p[:], node0[:], iota_col, ALU.add).then_inc(L.node_p_set, 1)
                    dve.tensor_scalar(rel[:, 0:nj], dcol[:, b, 0:nj], node0[:, 0:1], None, ALU.subtract)\
                       .then_inc(L.rel_set, 1)
                    if n == 1:
                        wait(dve, L.msg_set, o - 2)
                        dve.tensor_tensor(coef1[:, b, 0:nj, NBASE], dcol[:, b, 0:nj], dnext[:, b, 0:nj],
                                          ALU.not_equal).then_inc(L.last_set, 1)
                    if n == 1:
                        dve.wait_ge(L.rows_in[b], g.order2() * 32)
                        dve.wait_ge(L.node_p_set, o)
                        wait(dve, L.ex_done, o - 1)
                        turn = "p (j e) -> p j e" if g.tail else "p (e j) -> p j e"
                        dve.tensor_scalar(ST[:, 0:nj, :], dst_b[:, b, 0:nj * P].rearrange(turn, j=nj), node_p[:, 0:1],
                                          None, ALU.is_equal)
                        dve.tensor_scalar(typT[:, 0:nj, :], typ_b[:, b, 0:nj * P].rearrange(turn, j=nj),
                                          iota_col[0:NREL], None, ALU.is_equal).then_inc(L.prepared, 1)

                def one_hots(g):
                    b, nj, o = g.b, g.nj, g.order()
                    dve.wait_ge(L.rel_set, o)
                    wait(dve, L.summed, o - 2)
                    last = dve.tensor_tensor(S[:, b, 0:nj, :], rel[:, 0:nj].unsqueeze(2).broadcast_to([P, nj, P]),
                                             iota_row.unsqueeze(1).broadcast_to([P, nj, P]), ALU.is_equal)\
                              .then_inc(L.S_set, 1)

                def halves(v, nj):
                    return v.rearrange("p (h j) f -> p h j f", j=min(nj, 6))

                def scores(g):
                    nj, o = g.nj, g.order()
                    jj, hh = min(nj, 6), -(-nj // 6)
                    rows = ex_ps[:, 0:hh, 0:jj * KT].rearrange("p h (j k) -> p h j k", k=KT)
                    dve.wait_ge(L.gathered[g.q], g.gathers() * 16)
                    dve.wait_ge(L.ex_done, o)
                    dve.tensor_tensor(halves(prod[:, 0:nj, :], nj), halves(xg[:, g.q, 0:nj, :], nj), rows[:, :, :, 0:F],
                                      ALU.mult).then_inc(L.prod_set, 1)
                    dve.wait_ge(L.prod_set, o)
                    dve.tensor_reduce(dots[:, 0:nj], prod[:, 0:nj, :], AX_X, ALU.add).then_inc(L.dots_set, 1)
                    dve.wait_ge(L.dots_set, o)
                    two = "p (h j) -> p h j"
                    dve.tensor_tensor(score[:, 0:nj].rearrange(two, j=jj), dots[:, 0:nj].rearrange(two, j=jj),
                                      rows[:, :, :, F], ALU.add).then_inc(L.score_set, 1)

                def messages(g):
                    b, nj, o = g.b, g.nj, g.order()
                    if n == 1:
                        jj, hh = min(nj, 6), -(-nj // 6)
                        rows = ex_ps[:, 0:hh, 0:jj * KT].rearrange("p h (j k) -> p h j k", k=KT)
                        dve.wait_ge(L.att_set, o)
                        dve.tensor_tensor(halves(coef1[:, b, 0:nj, 0:NBASE], nj), rows[:, :, :, KA:KT],
                                          halves(att[:, 0:nj].unsqueeze(2).broadcast_to([P, nj, NBASE]), nj),
                                          ALU.mult).then_inc(L.coef_set, 1)
                        dve.wait_ge(L.coef_set, o)
                        dve.wait_ge(L.last_set, o)
                        coef = coef1[:, b, 0:nj, :]
                    else:
                        dve.wait_ge(L.coef_in[b], g.order2() * 16)
                        dve.wait_ge(L.gathered[g.q], g.gathers() * 16)
                        wait(dve, L.summed, o - 2)
                        coef = coef0[:, b, 0:nj, :]
                    dve.tensor_tensor(msg[:, b, 0:nj, 0:C * F].rearrange("p j (c f) -> p j c f", f=F),
                                      coef.unsqueeze(3).broadcast_to([P, nj, C, F]),
                                      xg[:, g.q, 0:nj, :].unsqueeze(2).broadcast_to([P, nj, C, F]),
                                      ALU.mult).then_inc(L.msg_set, 1)

                def add(g):
                    base = dve.value_load(bases[0:1, n, bass.ds(g.s, 1)], min_val=0, max_val=NPAD)
                    dve.wait_ge(L.projected, g.order())
                    wait(dve, L.added, g.order() - 1)
                    window = aggT[:, bass.ds(base, P)]
                    dve.tensor_tensor(window, window, outT_ps[g.b], ALU.add).then_inc(L.added, 1)

                def step(gs):
                    if n == 1 and gs[1]:
                        scores(gs[1])
                    if gs[0]:
                        prepare(gs[0])
                    if gs[3]:
                        add(gs[3])
                    if gs[1]:
                        messages(gs[1])
                    if gs[0]:
                        one_hots(gs[0])

                def one_pass(k):
                    if not isinstance(k, int):
                        dve.wait_ge(L.added, k * NG)
                        dve.tensor_scalar(moved[:, n:n + 1], moved[:, n:n + 1], float(P), None, ALU.add).then_inc(L.moved_on, 1)
                        dve.wait_ge(L.moved_on, k)
                        dve.tensor_scalar(bases[:, n, :], bases[:, n, :], float(P), float(NPAD), ALU.add, ALU.min)\
                           .then_inc(L.base_moved, 1)
                        dve.wait_ge(L.base_moved, k)
                    over_steps(dve, k, step, 3)

                dve.wait_ge(agg_cleared[n], 1)
                all_passes(dve, one_pass)

            dve.memset(zero[:], 0.0).then_inc(pad_zero, 1)
            dve.memset(moved[:], 0.0).then_inc(moved_zero, 1)
            dve.memset(eps[:], EPS).then_inc(eps_set, 1)
            dve.wait_ge(x_in, 16)
            for c in range(NCH):
                layernorm(0, c)
            dve.wait_ge(consts_in, 16)
            dve.tensor_tensor(ident[:], iota_row, iota_col.broadcast_to([P, P]), ALU.is_equal).then_inc(ident_set, 1)
            dve.wait_ge(weights_in, 128)
            dve.tensor_tensor(w0c[:], w0_sb[:], cg_sb[:], ALU.mult).then_inc(w0_set, 1)
            dve.tensor_scalar(relb_sb[:], relT_sb[:], a2b_sb[:, 0:1], None, ALU.add).then_inc(relb_set, 1)
            dve.wait_ge(rows_in, 16 * 6)
            dve.tensor_tensor(span[:], last_row[:], bases[:, 0, :], ALU.subtract).then_inc(span_set, 1)
            dve.wait_ge(span_set, 1)
            dve.tensor_reduce(span_max[:], span[:], AX_X, ALU.max).then_inc(span_max_set, 1)
            dve.wait_ge(span_max_set, 1)
            dve.tensor_scalar(beyond[:], span_max[:], float(P), None, ALU.is_ge).then_inc(beyond_set, 1)
            dve.wait_ge(moved_zero, 1)
            edge_work(0)
            dve.drain().then_inc(sums_done, 1)
            for c in range(NCH):
                dve.wait_ge(agg_turned, c + 1)
                xc = X[:, c * MC:(c + 1) * MC, :]
                dve.tensor_tensor(xc, xc, agg_ps[c % 2], ALU.add).then_inc(agg_used, 1)
                dve.wait_ge(agg_used, c + 1)
                layernorm(1, c)
            edge_work(1)
            dve.drain().then_inc(sums_done, 1)
            for c in range(NCH):
                dve.wait_ge(agg_turned, NCH + c + 1)
                xc = X[:, c * MC:(c + 1) * MC, :]
                dve.scalar_tensor_tensor(out=xc, in0=agg_ps[c % 2], scalar=0.0, in1=xc,
                                         op0=ALU.max, op1=ALU.add).then_inc(out_set, 1)


def _cg_table():
    import math
    combos = [(0, 0, 0), (0, 1, 1), (1, 0, 1), (1, 1, 0), (1, 1, 1), (2, 1, 1)]

    def coeff(j1, m1, j2, m2, j3, m3):
        if m3 != m1 + m2:
            return 0.0
        f = math.factorial
        vmin = max(0, j2 - j3 - m1, j1 + m2 - j3)
        vmax = min(j1 + j2 - j3, j1 - m1, j2 + m2)
        pref = (2 * j3 + 1) * f(j3 + j1 - j2) * f(j3 - j1 + j2) * f(j1 + j2 - j3) / f(j1 + j2 + j3 + 1)
        pref *= f(j3 + m3) * f(j3 - m3) * f(j1 - m1) * f(j1 + m1) * f(j2 - m2) * f(j2 + m2)
        total = 0.0
        for v in range(vmin, vmax + 1):
            total += (-1) ** v / (f(v) * f(j1 + j2 - j3 - v) * f(j1 - m1 - v) * f(j2 + m2 - v)
                                  * f(j3 - j2 + m1 + v) * f(j3 - j1 - m2 + v))
        return math.sqrt(pref) * total

    def su2(l1, l2, l3):
        c = np.zeros((2 * l1 + 1, 2 * l2 + 1, 2 * l3 + 1), dtype=np.complex128)
        for m1 in range(-l1, l1 + 1):
            for m2 in range(-l2, l2 + 1):
                if -l3 <= m1 + m2 <= l3:
                    c[m1 + l1, m2 + l2, m1 + m2 + l3] = coeff(l1, m1, l2, m2, l3, m1 + m2)
        return c

    def real(l):
        q = np.zeros((2 * l + 1, 2 * l + 1), dtype=np.complex128)
        for m in range(-l, 0):
            q[l + m, l + abs(m)] = 1 / np.sqrt(2)
            q[l + m, l - abs(m)] = -1j / np.sqrt(2)
        q[l, l] = 1.0
        for m in range(1, l + 1):
            q[l + m, l + abs(m)] = (-1) ** m / np.sqrt(2)
            q[l + m, l - abs(m)] = 1j * (-1) ** m / np.sqrt(2)
        return (-1j) ** l * q

    table = np.zeros((3 * P, F), np.float32)
    which = np.zeros((3 * P, F), np.int64)
    where_m = np.zeros((3 * P, F), np.int64)
    where_o = np.zeros((3 * P, F), np.int64)
    feature = {0: lambda m, j: m, 1: lambda m, j: 8 + 3 * m + j}
    first = {0: 0, 1: 1, 2: 4}
    for n, (le, ln, lo) in enumerate(combos):
        cg = np.einsum("ij,kl,mn,ikn->jlm", real(le), real(ln), np.conj(real(lo)).T, su2(le, ln, lo)).real
        cg = cg / np.linalg.norm(cg)
        for (i, j, k), value in np.ndenumerate(cg):
            for m in range(8):
                for o in range(8):
                    at = (first[le] + i) * F + feature[ln](m, j), feature[lo](o, k)
                    table[at], which[at], where_m[at], where_o[at] = value, n, m, o
    return table, which, where_m, where_o


def kernel(x, src, dst, edge_attr_3, edge_attr_5, edge_type_86, edge_weight1, L0_gnn_W, L1_gnn_weight, L1_gnn_w_comp,
           L1_gnn_self_loop_weight, L1_gnn_A1_w, L1_gnn_A1_b, L1_gnn_A2_w, L1_gnn_A2_b, L1_gnn_rel_emb):
    import concourse.bacc as _bacc
    from concourse.bass_utils import run_bass_kernel_spmd as _run

    def pad(a, n, value=0):
        a = np.asarray(a)
        return np.concatenate([a, np.full((n - a.shape[0],) + a.shape[1:], value, a.dtype)])

    table, which, where_m, where_o = _cg_table()
    arrays = {
        "x": pad(x, NPAD),
        "src": pad(src, EPAD),
        "dst": pad(dst, EPAD + 1, NOWHERE),
        "etype": pad(edge_type_86, EPAD),
        "edge": pad(np.concatenate([np.asarray(edge_weight1), np.asarray(edge_attr_3), np.asarray(edge_attr_5)], axis=1), EPAD),
        "ramp": np.concatenate([np.tile(np.arange(P, dtype=np.float32), (P, 1)),
                                np.arange(P, dtype=np.float32)[:, None]], axis=1),
        "cg": table,
        "w0": np.asarray(L0_gnn_W)[which, where_m, where_o],
        "w1": pad(np.concatenate([np.asarray(L1_gnn_weight).reshape(NBASE * F, F),
                                  np.asarray(L1_gnn_self_loop_weight)]), 5 * P),
        "a1b": np.concatenate([np.asarray(L1_gnn_A1_w), np.asarray(L1_gnn_A1_b)[:, None]], axis=1),
        "a2": np.asarray(L1_gnn_A2_w),
        "a2b": np.asarray(L1_gnn_A2_b)[:, None],
        "relT": np.ascontiguousarray(np.asarray(L1_gnn_rel_emb).T),
        "wcomp": np.asarray(L1_gnn_w_comp),
    }
    arrays = {f"in_{k}_dram": np.ascontiguousarray(v) for k, v in arrays.items()}
    nc = _bacc.Bacc("TRN2", target_bir_lowering=False, num_devices=1)
    args = [nc.dram_tensor(k, v.shape, mybir.dt.from_np(v.dtype), kind="ExternalInput").ap() for k, v in arrays.items()]
    args.append(nc.dram_tensor("out_0_dram", (N, F), F32, kind="ExternalOutput").ap())
    build(nc, *args)
    r = _run(nc, [arrays], core_ids=[0])
    return r.results[0]["out_0_dram"]
```

```python
import concourse.bass as bass
from concourse import mybir
from contextlib import ExitStack
import numpy as np

F32 = mybir.dt.float32
I32 = mybir.dt.int32
BF16 = mybir.dt.bfloat16
ALU = mybir.AluOpType
ACT = mybir.ActivationFunctionType
AX_X = mybir.AxisListType.X

N, F = 12500, 32
E = 200000
NREL, NBASE = 86, 16
P = 128
M = -(-N // P)
NPAD = M * P
NWIN = NPAD + P
J = 12
GE = P * J
FULL = E // GE
JT = -(-(E - FULL * GE) // P)
NG = FULL + 1
T = FULL * J + JT
EPAD = T * P
WN = 16
JH = J // 2
HW = JH * WN
NCH = 7
MC = M // NCH
KA = F + 1
KT = KA + NBASE
C0, C1 = 9, 17
PASSES = -(-N // WN)
QS = [[0, 3, 5, 7, 9], [0, 5, 9, 13, 17]]
CQ = [3, 5]
NOWHERE = 1 << 20
EPS = 1e-5
assert NCH * MC == M and FULL % 2 == 0 and JT <= JH


class Group:

    def __init__(self, i, r, k):
        self.i, self.r, self.k = i, r, k
        self.b = r % 2
        self.q = r % 4
        self.s = i * 4 + r
        self.tail = isinstance(self.s, int) and self.s == FULL
        self.nj = JT if self.tail else J

    def order(self):
        return self.k * NG + self.s + 1

    def order2(self):
        return self.k * len(range(self.b, NG, 2)) + self.i * 2 + self.r // 2 + 1

    def order4(self):
        return self.k * len(range(self.q, NG, 4)) + self.i + self.r // 4 + 1

    def halves(self):
        return -(-self.nj // JH), min(self.nj, JH) * WN

    def gathers(self):
        a_pass = len(range(self.q, NG, 4)) * J
        if self.q == FULL % 4:
            a_pass -= J - JT
        if self.tail:
            return (self.k + 1) * a_pass
        return self.k * a_pass + self.i * J + (self.r // 4 + 1) * J


def wait(eng, sem, n):
    if not isinstance(n, int) or n > 0:
        eng.wait_ge(sem, n)


def over_steps(eng, k, body, lag):
    def step(i, r):
        body([Group(i, r - d, k) if not isinstance(i, int) or 0 <= i * 4 + r - d < NG else None for d in range(lag + 1)])
    for t in range(4):
        step(0, t)
    with eng.Fori(0, FULL // 4 - 1) as i:
        for u in range(4):
            step(i, 4 + u)
    for t in range(FULL // 4 * 4, NG + lag):
        step(0, t)


def build(nc, x, src_t, dst_t, dnext_t, dst, etype, edge, tile_first, tile_last, group_first, group_last, group_of_tile,
          place_first, ramp, cg, w0, w1, a1b, a2, a2b, relT, wcomp, out):
    h_table = [nc.dram_tensor(f"h_table{n}", (NPAD, F), F32).ap() for n in range(2)]
    p_table = nc.dram_tensor("p_table", (NWIN, 3 * KA), BF16).ap()

    with ExitStack() as ctx:
        def sb(name, shape, dt=F32):
            return ctx.enter_context(nc.sbuf_tensor(name, shape, dt))

        def sem(name):
            return ctx.enter_context(nc.semaphore(name))

        ps = ctx.enter_context(nc.psum_tensor("ps", [P, 8, 512], F32))
        G_ps = ps[:, 0:2, :]
        ex_ps = ps[:, 2:4, :]
        oT_ps = ps[0:F, 4, :]
        o_ps = ps[0:HW, 5, 0:2 * F].rearrange("p (h o) -> p h o", h=2)
        win_ps = ps[0:F, 6, 0:P]
        agg_ps = [ps[:, b, 0:MC * F].rearrange("p (m f) -> p m f", f=F) for b in range(2)]
        hT_ps = ps[0:F, 2:6, :].rearrange("p b n -> p (b n)")
        p_ps = [ps[:, 6 + b, 0:MC * KA] for b in range(2)]

        ramp_sb = sb("ramp_sb", [P, P + 2])
        iota_row, iota_col, node_in_tile = ramp_sb[:, 0:P], ramp_sb[:, P:P + 1], ramp_sb[0:HW, P + 1:P + 2]
        ident = sb("ident", [P, P])
        zero = sb("zero", [P, 3 * KA], BF16)
        eps = sb("eps", [P, 1])
        cg_sb = sb("cg_sb", [P, CQ[0], F])
        w0_sb = sb("w0_sb", [P, CQ[0], F])
        w0c = sb("w0c", [P, CQ[0], F])
        w1_sb = sb("w1_sb", [P, CQ[1], F])
        a1b_sb = sb("a1b_sb", [F, KA])
        a2_sb = sb("a2_sb", [F, F])
        a2b_sb = sb("a2b_sb", [F, 1])
        relT_sb = sb("relT_sb", [F, NREL])
        relb_sb = sb("relb_sb", [F, NREL])
        p_w = sb("p_w", [F, KA])
        rel_tab = sb("rel_tab", [NREL, KT])
        rel_left = sb("rel_left", [NREL, KT])
        rel_3 = sb("rel_3", [NREL, 3, KT], BF16)

        X = sb("X", [P, M, F])
        H = sb("H", [P, 2, MC, F])
        centred = sb("centred", [P, MC, F])
        squares = sb("squares", [P, MC, F])
        row_sum = sb("row_sum", [P, MC])
        row_var = sb("row_var", [P, MC])
        row_std = sb("row_std", [P, MC])
        row_rstd = sb("row_rstd", [P, MC])
        hT = sb("hT", [F, MC * P])
        p_left = sb("p_left", [P, MC, KA])
        p_rows = sb("p_rows", [P, 2, MC, 3, KA], BF16)
        aggT = sb("aggT", [F, NWIN])

        bases = sb("bases", [1, 2, NG], I32)
        node_all = sb("node_all", [P, 2, NG])
        rel_all = sb("rel_all", [P, T])
        rel_group = sb("rel_group", [P, T])
        last_all = sb("last_all", [P, T])
        place = sb("place", [HW, NG, 2])
        span_max = sb("span_max", [1, 2])
        too_wide = sb("too_wide", [1, 2])
        beyond = sb("beyond", [1, 1], I32)

        idx = sb("idx", [P, 2, J], I32)
        coef0 = sb("coef0", [P, 2, J, C0])
        dst_b = sb("dst_b", [P, 2, GE], I32)
        typ_b = sb("typ_b", [NREL, 2, GE], I32)
        p_win = sb("p_win", [P, 2, 3, KA], BF16)
        xg = sb("xg", [P, 4, J, F])
        S = sb("S", [P, 2, J, WN])
        dstT = sb("dstT", [P, J, P], BF16)
        typT = sb("typT", [NREL, J, P], BF16)
        prod = sb("prod", [P, J, F])
        dots = sb("dots", [P, J])
        score = sb("score", [P, J])
        score_r = sb("score_r", [P, J])
        att = sb("att", [P, J])
        coef1 = sb("coef1", [P, 2, J, C1])
        Z = sb("Z", [P, 2, J, C1 * WN])
        R = sb("R", [HW, 2, 2, P])
        G_sb = sb("G_sb", [P, CQ[1], 2, HW])
        oT_sb = sb("oT_sb", [F, 2, HW])
        o_sb = sb("o_sb", [HW, 2, F])

        room = Z[:].rearrange("p b j z -> p (b j z)").bitcast(I32)
        dst_all, dnext_all, first_all, group_all = (room[:, i * T:(i + 1) * T] for i in range(4))
        wide = dst_b[:].rearrange("p b e -> p (b e)")
        base_all, place_all = wide[:, 0:NG], wide[0:HW, NG:3 * NG].rearrange("p (g h) -> p g h", h=2)
        rows = typ_b[0:1].rearrange("p b e -> p (b e)")
        group_row = [rows[:, i * NG:(i + 1) * NG] for i in range(2)]
        span = squares[0:1].rearrange("p m f -> p (m f)")[:, 0:NG]
        tile_row = [rows[:, 2 * NG:2 * NG + T], sb("tile_span", [1, T], I32)[:]]

        consts_in, weights_in, x_in, windows_in = sem("consts_in"), sem("weights_in"), sem("x_in"), sem("windows_in")
        out_done, pad_done = sem("out_done"), sem("pad_done")
        pad_zero, eps_set = sem("pad_zero"), sem("eps_set")
        ident_set, w0_set, relb_set = sem("ident_set"), sem("w0_set"), sem("relb_set")
        rel_left_set, rel_3_set = sem("rel_left_set"), sem("rel_3_set")
        span_set, span_max_set, wide_set, beyond_set = sem("span_set"), sem("span_max_set"), sem("wide_set"), sem("beyond_set")
        windows_set, place_set = sem("windows_set"), sem("place_set")
        pw_ps_ready, pw_set = sem("pw_ps_ready"), sem("pw_set")
        sum_set, centred_set, squares_set, var_set = sem("sum_set"), sem("centred_set"), sem("squares_set"), sem("var_set")
        std_set, rstd_set, h_set = sem("std_set"), sem("rstd_set"), sem("h_set")
        h_stored = [[sem(f"h_stored{n}_{b}") for b in range(2)] for n in range(2)]
        agg_turned, sums_done, out_set = sem("agg_turned"), sem("sums_done"), sem("out_set")
        agg_used = sem("agg_used")
        agg_cleared = [sem("agg_cleared0"), sem("agg_cleared1")]
        h_turned, hT_set, p_mm = sem("h_turned"), sem("hT_set"), sem("p_mm")
        p_high_set, p_left_set, p_mid_set, p_set = sem("p_high_set"), sem("p_left_set"), sem("p_mid_set"), sem("p_set")
        p_stored = [sem(f"p_stored{b}") for b in range(2)]

        class Edge:

            def __init__(self, n):
                self.idx_in = [sem(f"idx_in{n}_{b}") for b in range(2)]
                self.coef_in = [sem(f"coef_in{n}_{b}") for b in range(2)]
                self.rows_in = [sem(f"rows_in{n}_{b}") for b in range(2)]
                self.pwin_in = [sem(f"pwin_in{n}_{b}") for b in range(2)]
                self.gathered = [sem(f"gathered{n}_{q}") for q in range(4)]
                self.gather_go = sem(f"gather_go{n}")
                self.load_go = sem(f"load_go{n}")
                self.turn_go = sem(f"turn_go{n}")
                self.S_set = sem(f"S_set{n}")
                self.last_set = sem(f"last_set{n}")
                self.dstT_set = sem(f"dstT_set{n}")
                self.typT_set = sem(f"typT_set{n}")
                self.ex_done = sem(f"ex_done{n}")
                self.prod_set = sem(f"prod_set{n}")
                self.dots_set = sem(f"dots_set{n}")
                self.score_set = sem(f"score_set{n}")
                self.score_r_set = sem(f"score_r_set{n}")
                self.att_set = sem(f"att_set{n}")
                self.coef_set = sem(f"coef_set{n}")
                self.Z_set = sem(f"Z_set{n}")
                self.R_set = sem(f"R_set{n}")
                self.summed = sem(f"summed{n}")
                self.G_set = sem(f"G_set{n}")
                self.projected = sem(f"projected{n}")
                self.oT_set = sem(f"oT_set{n}")
                self.turned = sem(f"turned{n}")
                self.o_set = sem(f"o_set{n}")
                self.placed = sem(f"placed{n}")
                self.added = sem(f"added{n}")
                self.restarted = sem(f"restarted{n}")
                self.moved_on = sem(f"moved_on{n}")

        layers = [Edge(0), Edge(1)]
        block = ctx.enter_context(nc.Block())

        def all_passes(eng, passes, restart=None):
            passes(0)
            eng.wait_ge(beyond_set, 1)
            too_far = eng.value_load(beyond[0:1, 0:1], min_val=0, max_val=1)
            with eng.If(too_far):
                if restart:
                    restart()
                with eng.Fori(1, PASSES + 1) as k:
                    passes(k)

        @block.sync
        def _(sp):
            sp.dma_start(X[:], x.rearrange("(p m) f -> p m f", m=M)).then_inc(x_in, 16)
            sp.dma_start(ramp_sb[:], ramp).then_inc(consts_in, 16)
            for to, of in ((dst_all, dst_t), (dnext_all, dnext_t), (first_all, tile_first.partition_broadcast(P)),
                           (group_all, group_of_tile.partition_broadcast(P)), (base_all, group_first.partition_broadcast(P)),
                           (place_all, place_first), (tile_row[0], tile_first.rearrange("(a t) -> a t", a=1)),
                           (tile_row[1], tile_last.rearrange("(a t) -> a t", a=1)),
                           (group_row[0], group_first.rearrange("(a t) -> a t", a=1)),
                           (group_row[1], group_last.rearrange("(a t) -> a t", a=1)),
                           (bases[:, 0, :], group_first.rearrange("(a t) -> a t", a=1)),
                           (bases[:, 1, :], group_first.rearrange("(a t) -> a t", a=1))):
                sp.dma_start(to, of).then_inc(windows_in, 16)
            for to, of in ((cg_sb[:], cg), (w0_sb[:], w0), (w1_sb[:], w1), (a1b_sb[:], a1b), (a2_sb[:], a2), (a2b_sb[:], a2b),
                           (relT_sb[:], relT), (rel_tab[:, KA:KT], wcomp)):
                sp.dma_start(to, of).then_inc(weights_in, 16)
            sp.wait_ge(pad_zero, 1)
            sp.dma_start(p_table[NPAD:NWIN, :], zero[:]).then_inc(pad_done, 16)

            def store_h(n, c):
                table = h_table[n].rearrange("(p m) f -> p m f", m=M)
                sp.wait_ge(h_set, n * NCH + c + 1)
                sp.dma_start(table[:, c * MC:(c + 1) * MC, :], H[:, c % 2]).then_inc(h_stored[n][c % 2], 16)

            def store_p(c):
                table = p_table[0:NPAD, :].rearrange("(p m) k -> p m k", m=M)
                sp.wait_ge(p_set, c + 1)
                sp.dma_start(table[:, c * MC:(c + 1) * MC, :],
                             p_rows[:, c % 2].rearrange("p m a k -> p m (a k)")).then_inc(p_stored[c % 2], 16)

            def edge_loads(n):
                L = layers[n]

                def loads(g):
                    b, nj = g.b, g.nj
                    if isinstance(g.s, int) and g.s < 2:
                        if not isinstance(g.k, int):
                            sp.wait_ge(L.added, g.k * NG)
                            sp.nop().then_inc(L.load_go, 1)
                            sp.wait_ge(L.moved_on, g.k * 3)
                            sp.nop().then_inc(L.load_go, 1)
                    else:
                        back = Group(g.i, g.r - 2, g.k)
                        sp.wait_ge(L.gathered[back.q], back.gathers() * 16)
                        sp.nop().then_inc(L.load_go, 1)
                    tiles = slice(FULL * J, T) if g.tail else bass.ds(g.s * J, J)
                    edges = slice(FULL * GE, EPAD) if g.tail else bass.ds(g.s * GE, GE)
                    if n == 1:
                        base = sp.value_load(bases[0:1, n, bass.ds(g.s, 1)], min_val=0, max_val=NPAD)
                    sp.dma_start(idx[:, b, 0:nj], src_t[:, tiles]).then_inc(L.idx_in[b], 16)
                    if n == 1:
                        wait(sp, L.typT_set, g.order() - 2)
                        sp.nop().then_inc(L.load_go, 1)
                        sp.dma_start(dst_b[:, b, 0:nj * P], dst[edges].partition_broadcast(P)).then_inc(L.rows_in[b], 16)
                        sp.dma_start(typ_b[:, b, 0:nj * P], etype[edges].partition_broadcast(NREL)).then_inc(L.rows_in[b], 16)
                        wait(sp, L.ex_done, g.order() - 2)
                        sp.nop().then_inc(L.load_go, 1)
                        sp.dma_start(p_win[:, b].rearrange("p a k -> p (a k)"), p_table[bass.ds(base, P), :])\
                          .then_inc(L.pwin_in[b], 16)
                    else:
                        wait(sp, L.Z_set, g.order() - 2)
                        sp.nop().then_inc(L.load_go, 1)
                        sp.dma_start(coef0[:, b, 0:nj, :], edge[:, tiles, :]).then_inc(L.coef_in[b], 16)

                all_passes(sp, lambda k: over_steps(sp, k, lambda gs: loads(gs[0]), 0))

            for c in range(NCH):
                store_h(0, c)
            edge_loads(0)
            for c in range(NCH + 1):
                if c < NCH:
                    store_h(1, c)
                if c >= 1:
                    store_p(c - 1)
            for b in range(2):
                sp.wait_ge(p_stored[b], 16 * len(range(b, NCH, 2)))
            sp.wait_ge(pad_done, 16)
            edge_loads(1)
            left = N - (P - 1) * M
            rows = out[0:(P - 1) * M, :].rearrange("(p m) f -> p m f", m=M)
            rest = out[(P - 1) * M:N, :].rearrange("(a m) f -> a m f", a=1)
            stores = 0
            for c in range(NCH):
                lo, hi = c * MC, (c + 1) * MC
                sp.wait_ge(out_set, c + 1)
                sp.dma_start(rows[0:112, lo:hi, :], X[0:112, lo:hi, :]).then_inc(out_done, 16)
                sp.dma_start(rows[112:P - 1, lo:hi, :], X[112:P - 1, lo:hi, :]).then_inc(out_done, 16)
                stores += 2
                if lo < left:
                    sp.dma_start(rest[:, lo:min(hi, left), :], X[P - 1:P, lo:min(hi, left), :]).then_inc(out_done, 16)
                    stores += 1
            sp.wait_ge(out_done, 16 * stores)

        @block.gpsimd
        def _(pool):
            def edge_gathers(n):
                L = layers[n]

                def gather(g):
                    pool.wait_ge(L.idx_in[g.b], g.order2() * 16)
                    pool.nop().then_inc(L.gather_go, 1)
                    wait(pool, L.summed, g.order() - 4)
                    pool.nop().then_inc(L.gather_go, 1)
                    for j in range(g.nj):
                        pool.indirect_dma_start(
                            xg[:, g.q, j, :], None, h_table[n],
                            bass.IndirectOffsetOnAxis(ap=idx[:, g.b, j:j + 1], axis=0)).then_inc(L.gathered[g.q], 16)

                all_passes(pool, lambda k: over_steps(pool, k, lambda gs: gather(gs[0]), 0))

            pool.memset(aggT[:], 0.0).then_inc(agg_cleared[0], 1)
            for b in range(2):
                pool.wait_ge(h_stored[0][b], 16 * len(range(b, NCH, 2)))
            edge_gathers(0)
            pool.wait_ge(agg_turned, NCH)
            pool.memset(aggT[:], 0.0).then_inc(agg_cleared[1], 1)
            for b in range(2):
                pool.wait_ge(h_stored[1][b], 16 * len(range(b, NCH, 2)))
            edge_gathers(1)

        @block.tensor
        def _(pe):
            def turn_agg(n, c):
                wait(pe, out_set if n else agg_used, c - 1)
                for m in range(MC):
                    at = c * MC + m
                    last = pe.transpose(agg_ps[c % 2][:, m, :], aggT[:, at:at + M * (P - 1) + 1:M], ident[0:F, 0:F])
                last.then_inc(agg_turned, 1)

            def node_tables(c):
                pe.wait_ge(h_set, NCH + c + 1)
                wait(pe, hT_set, c)
                for m in range(MC):
                    last = pe.transpose(hT_ps[:, m * P:(m + 1) * P], H[:, c % 2, m, :], ident[:])
                last.then_inc(h_turned, 1)
                pe.wait_ge(hT_set, c + 1)
                wait(pe, p_left_set, c - 1)
                for m in range(MC):
                    last = pe.matmul(p_ps[c % 2][:, m * KA:(m + 1) * KA], hT[:, m * P:(m + 1) * P], p_w[:],
                                     start=True, stop=True)
                last.then_inc(p_mm, 1)

            def edge_sums(n):
                L = layers[n]
                qs, cq = QS[n], CQ[n]
                weights = w0c if n == 0 else w1_sb

                def attention_rows(g):
                    pe.wait_ge(L.typT_set, g.order())
                    pe.wait_ge(L.pwin_in[g.b], g.order2() * 16)
                    wait(pe, L.coef_set, g.order() - 1)
                    for j in range(g.nj):
                        to = ex_ps[:, j // JH, j % JH * KT:j % JH * KT + KT]
                        for a in range(3):
                            pe.matmul(to, typT[:, j, :], rel_3[:, a, :], start=(a == 0), stop=False)
                        for a in range(3):
                            last = pe.matmul(to[:, 0:KA], dstT[:, j, :], p_win[:, g.b, a, :], start=False, stop=(a == 2))
                    last.then_inc(L.ex_done, 1)

                def project(g):
                    hh, w = g.halves()
                    pe.wait_ge(L.G_set, g.order())
                    wait(pe, L.oT_set, g.order() - 1)
                    for c in range(cq):
                        rows = P if c < cq - 1 else F
                        last = pe.matmul(oT_ps[:, 0:hh * w], weights[0:rows, c, :], G_sb[0:rows, c, 0:hh, 0:w],
                                         start=(c == 0), stop=(c == cq - 1))
                    last.then_inc(L.projected, 1)

                def turn(g):
                    hh, w = g.halves()
                    pe.wait_ge(L.oT_set, g.order())
                    wait(pe, L.o_set, g.order() - 1)
                    pe.nop().then_inc(L.turn_go, 1)
                    for h in range(hh):
                        last = pe.transpose(o_ps[0:w, h, :], oT_sb[:, h, 0:w], ident[0:F, 0:F])
                    last.then_inc(L.turned, 1)

                def place_rows(g):
                    hh, w = g.halves()
                    pe.wait_ge(L.o_set, g.order())
                    pe.wait_ge(L.R_set, g.order())
                    wait(pe, L.added, g.order() - 1)
                    pe.nop().then_inc(L.turn_go, 1)
                    for h in range(hh):
                        last = pe.matmul(win_ps, o_sb[0:w, h, :], R[0:w, g.b, h, :], start=(h == 0), stop=(h == hh - 1))
                    last.then_inc(L.placed, 1)

                def sum_edges(g, back):
                    wait(pe, L.G_set, g.order() - 1)
                    pe.wait_ge(L.gathered[g.q], g.gathers() * 16)
                    pe.wait_ge(L.Z_set, g.order())
                    for j in range(g.nj):
                        bank = G_ps[:, j // JH, 0:cq * HW].rearrange("p (c j n) -> p c j n", c=cq, j=JH)
                        for q in range(4):
                            last = pe.matmul(bank[q * F:(q + 1) * F, 0:qs[q + 1] - qs[q], j % JH, :], xg[:, g.q, j, :],
                                             Z[:, g.b, j, qs[q] * WN:qs[q + 1] * WN], start=True, stop=True,
                                             tile_position=(0, q * F))
                        if j == g.nj - 1:
                            last.then_inc(L.summed, 1)
                        if back and j == min(g.nj, J // 3) - 1:
                            turn(back)
                        if back and j == min(g.nj, 2 * J // 3) - 1:
                            place_rows(back)

                def step(gs):
                    if n == 1 and gs[0]:
                        attention_rows(gs[0])
                    if gs[2]:
                        project(gs[2])
                    if gs[1]:
                        sum_edges(gs[1], gs[2])
                    elif gs[2]:
                        turn(gs[2])
                        place_rows(gs[2])

                all_passes(pe, lambda k: over_steps(pe, k, step, 2))

            pe.wait_ge(weights_in, 128)
            pe.wait_ge(relb_set, 1)
            pe.matmul(ps[0:F, 6, 0:KA], a2_sb[:], a1b_sb[:], start=True, stop=True)
            pe.matmul(ps[0:NREL, 7, 0:KA], relb_sb[:], a1b_sb[:], start=True, stop=True).then_inc(pw_ps_ready, 1)
            pe.wait_ge(ident_set, 1)
            pe.wait_ge(w0_set, 1)
            pe.wait_ge(pw_set, 2)
            edge_sums(0)
            pe.wait_ge(sums_done, 1)
            for c in range(NCH + 1):
                if c < NCH:
                    turn_agg(0, c)
                if c >= 1:
                    node_tables(c - 1)
            pe.wait_ge(p_set, NCH)
            pe.wait_ge(rel_3_set, 3)
            edge_sums(1)
            pe.wait_ge(sums_done, 2)
            for c in range(NCH):
                turn_agg(1, c)

        @block.scalar
        def _(act):
            def std(n):
                for c in range(NCH):
                    act.wait_ge(var_set, n * NCH + c + 1)
                    act.activation(row_std[:], row_var[:], ACT.Sqrt, bias=eps[:, 0:1], scale=1.0 / F).then_inc(std_set, 1)
                    if n == 1:
                        act.wait_ge(h_turned, c + 1)
                        wait(act, p_mm, c)
                        act.activation(hT[:], hT_ps[:, 0:MC * P], ACT.Copy).then_inc(hT_set, 1)
                        act.wait_ge(p_mm, c + 1)
                        if c >= 2:
                            act.wait_ge(p_stored[c % 2], 16 * (c // 2))
                        act.activation(p_rows[:, c % 2, :, 0, :], p_ps[c % 2].rearrange("p (m k) -> p m k", k=KA),
                                       ACT.Copy).then_inc(p_high_set, 1)

            def edge_copies(n):
                L = layers[n]
                cq = CQ[n]

                def attention(g):
                    act.wait_ge(L.score_set, g.order())
                    act.activation(score_r[:, 0:g.nj], score[:, 0:g.nj], ACT.Relu).then_inc(L.score_r_set, 1)
                    act.wait_ge(L.score_r_set, g.order())
                    act.activation(att[:, 0:g.nj], score_r[:, 0:g.nj], ACT.Tanh, scale=float(F) ** -0.5)\
                       .then_inc(L.att_set, 1)

                def copy_G(g):
                    hh, w = g.halves()
                    act.wait_ge(L.summed, g.order())
                    wait(act, L.projected, g.order() - 1)
                    bank = G_ps[:, 0:hh, 0:cq * HW].rearrange("p h (c w) -> p h c w", c=cq)
                    to = G_sb[:, 0:cq, 0:hh, 0:w].rearrange("p c h w -> p h c w")
                    act.activation(to[0:F, :, cq - 1, :], bank[0:F, :, cq - 1, 0:w], ACT.Copy)
                    act.activation(to[:, :, 0:cq - 1, :], bank[:, :, 0:cq - 1, 0:w], ACT.Copy).then_inc(L.G_set, 1)

                def copy_oT(g):
                    hh, w = g.halves()
                    act.wait_ge(L.projected, g.order())
                    wait(act, L.turned, g.order() - 1)
                    act.activation(oT_sb[:, 0:hh, 0:w], oT_ps[:, 0:hh * w].rearrange("p (h w) -> p h w", h=hh),
                                   ACT.Copy).then_inc(L.oT_set, 1)

                def copy_o(g):
                    hh, w = g.halves()
                    act.wait_ge(L.turned, g.order())
                    wait(act, L.placed, g.order() - 1)
                    act.activation(o_sb[0:w, 0:hh, :], o_ps[0:w, 0:hh, :], ACT.Copy).then_inc(L.o_set, 1)

                def step(gs):
                    if n == 1 and gs[1]:
                        attention(gs[1])
                    if gs[2]:
                        copy_G(gs[2])
                        copy_oT(gs[2])
                        copy_o(gs[2])

                all_passes(act, lambda k: over_steps(act, k, step, 2))

            act.wait_ge(eps_set, 1)
            std(0)
            act.wait_ge(pw_ps_ready, 1)
            act.activation(p_w[:], ps[0:F, 6, 0:KA], ACT.Copy).then_inc(pw_set, 1)
            act.activation(rel_tab[:, 0:KA], ps[0:NREL, 7, 0:KA], ACT.Copy).then_inc(pw_set, 1)
            edge_copies(0)
            std(1)
            edge_copies(1)

        @block.vector
        def _(dve):
            def layernorm(n, c):
                o = n * NCH + c + 1
                xc = X[:, c * MC:(c + 1) * MC, :]
                dve.tensor_reduce(row_sum[:], xc, AX_X, ALU.add).then_inc(sum_set, 1)
                dve.wait_ge(sum_set, o)
                dve.scalar_tensor_tensor(out=centred[:], in0=row_sum[:].unsqueeze(2).broadcast_to([P, MC, F]), scalar=-1.0 / F,
                                         in1=xc, op0=ALU.mult, op1=ALU.add).then_inc(centred_set, 1)
                dve.wait_ge(centred_set, o)
                dve.tensor_tensor(squares[:], centred[:], centred[:], ALU.mult).then_inc(squares_set, 1)
                dve.wait_ge(squares_set, o)
                dve.tensor_reduce(row_var[:], squares[:], AX_X, ALU.add).then_inc(var_set, 1)
                dve.wait_ge(std_set, o)
                dve.reciprocal(row_rstd[:], row_std[:]).then_inc(rstd_set, 1)
                dve.wait_ge(rstd_set, o)
                if c >= 2:
                    dve.wait_ge(h_stored[n][c % 2], 16 * (c // 2))
                    if n == 1:
                        dve.wait_ge(h_turned, c - 1)
                dve.scalar_tensor_tensor(out=H[:, c % 2], in0=centred[:], scalar=0.0,
                                         in1=row_rstd[:].unsqueeze(2).broadcast_to([P, MC, F]),
                                         op0=ALU.max, op1=ALU.mult).then_inc(h_set, 1)

            def split_p(c):
                dve.wait_ge(p_high_set, c + 1)
                wait(dve, p_set, c)
                dve.tensor_tensor(p_left[:], p_ps[c % 2].rearrange("p (m k) -> p m k", k=KA), p_rows[:, c % 2, :, 0, :],
                                  ALU.subtract).then_inc(p_left_set, 1)
                dve.wait_ge(p_left_set, c + 1)
                dve.tensor_copy(p_rows[:, c % 2, :, 1, :], p_left[:]).then_inc(p_mid_set, 1)
                dve.wait_ge(p_mid_set, c + 1)
                dve.tensor_tensor(p_rows[:, c % 2, :, 2, :], p_left[:], p_rows[:, c % 2, :, 1, :],
                                  ALU.subtract).then_inc(p_set, 1)

            def edge_work(n):
                L = layers[n]
                C = C0 if n == 0 else C1

                def tiles(v, g):
                    return v[:, FULL * J:T] if g.tail else v[:, bass.ds(g.s * J, J)]

                def one_hots(g):
                    b, nj, o = g.b, g.nj, g.order()
                    wait(dve, L.Z_set, o - 2)
                    dve.tensor_tensor(S[:, b, 0:nj, :], tiles(rel_all, g).unsqueeze(2).broadcast_to([P, nj, WN]),
                                      iota_row[:, 0:WN].unsqueeze(1).broadcast_to([P, nj, WN]), ALU.is_equal)\
                       .then_inc(L.S_set, 1)
                    if n == 1:
                        dve.tensor_copy(coef1[:, b, 0:nj, NBASE], tiles(last_all, g)).then_inc(L.last_set, 1)
                        dve.wait_ge(L.rows_in[b], g.order2() * 32)
                        wait(dve, L.ex_done, o - 1)
                        node = node_all[:, n, FULL:NG] if g.tail else node_all[:, n, bass.ds(g.s, 1)]
                        dve.tensor_scalar(dstT[:, 0:nj, :].rearrange("p j e -> p (j e)"), dst_b[:, b, 0:nj * P], node, None,
                                          ALU.is_equal).then_inc(L.dstT_set, 1)
                        dve.wait_ge(L.dstT_set, o)
                        dve.tensor_scalar(typT[:, 0:nj, :].rearrange("p j e -> p (j e)"), typ_b[:, b, 0:nj * P],
                                          iota_col[0:NREL], None, ALU.is_equal).then_inc(L.typT_set, 1)

                def banks(v, nj):
                    return v.rearrange("p (h j) f -> p h j f", j=min(nj, JH))

                def ex_rows(nj):
                    return ex_ps[:, 0:-(-nj // JH), 0:min(nj, JH) * KT].rearrange("p h (j k) -> p h j k", k=KT)

                def scores(g):
                    nj, o = g.nj, g.order()
                    rows = ex_rows(nj)
                    dve.wait_ge(L.gathered[g.q], g.gathers() * 16)
                    dve.wait_ge(L.ex_done, o)
                    dve.tensor_tensor(banks(prod[:, 0:nj, :], nj), banks(xg[:, g.q, 0:nj, :], nj), rows[:, :, :, 0:F],
                                      ALU.mult).then_inc(L.prod_set, 1)
                    dve.wait_ge(L.prod_set, o)
                    dve.tensor_reduce(dots[:, 0:nj], prod[:, 0:nj, :], AX_X, ALU.add).then_inc(L.dots_set, 1)
                    dve.wait_ge(L.dots_set, o)
                    two, jj = "p (h j) -> p h j", min(nj, JH)
                    dve.tensor_tensor(score[:, 0:nj].rearrange(two, j=jj), dots[:, 0:nj].rearrange(two, j=jj),
                                      rows[:, :, :, F], ALU.add).then_inc(L.score_set, 1)

                def coefficients(g):
                    nj = g.nj
                    dve.wait_ge(L.att_set, g.order())
                    dve.tensor_tensor(banks(coef1[:, g.b, 0:nj, 0:NBASE], nj), ex_rows(nj)[:, :, :, KA:KT],
                                      banks(att[:, 0:nj].unsqueeze(2).broadcast_to([P, nj, NBASE]), nj),
                                      ALU.mult).then_inc(L.coef_set, 1)

                def spread(g):
                    b, nj, o = g.b, g.nj, g.order()
                    if n == 0:
                        dve.wait_ge(L.coef_in[b], g.order2() * 16)
                        coef = coef0[:, b, 0:nj, :]
                    else:
                        dve.wait_ge(L.coef_set, o)
                        dve.wait_ge(L.last_set, o)
                        coef = coef1[:, b, 0:nj, :]
                    dve.wait_ge(L.S_set, o)
                    wait(dve, L.summed, o - 2)
                    dve.tensor_tensor(Z[:, b, 0:nj, 0:C * WN].rearrange("p j (c n) -> p j c n", n=WN),
                                      coef.unsqueeze(3).broadcast_to([P, nj, C, WN]),
                                      S[:, b, 0:nj, :].unsqueeze(2).broadcast_to([P, nj, C, WN]),
                                      ALU.mult).then_inc(L.Z_set, 1)
                    hh, w = g.halves()
                    wait(dve, L.placed, o - 2)
                    at = place[0:w, FULL, 0:hh] if g.tail else place[0:w, bass.ds(g.s, 1), :].rearrange("p a h -> p (a h)")
                    dve.tensor_tensor(R[0:w, b, 0:hh, :], at.unsqueeze(2).broadcast_to([w, hh, P]),
                                      iota_row[0:w].unsqueeze(1).broadcast_to([w, hh, P]), ALU.is_equal)\
                       .then_inc(L.R_set, 1)

                def add(g):
                    base = dve.value_load(bases[0:1, n, bass.ds(g.s, 1)], min_val=0, max_val=NPAD)
                    dve.wait_ge(L.placed, g.order())
                    wait(dve, L.added, g.order() - 1)
                    window = aggT[:, bass.ds(base, P)]
                    dve.tensor_tensor(window, window, win_ps, ALU.add).then_inc(L.added, 1)

                def step(gs):
                    if n == 1 and gs[1]:
                        scores(gs[1])
                    if gs[0]:
                        one_hots(gs[0])
                    if n == 1 and gs[1]:
                        coefficients(gs[1])
                    if gs[3]:
                        add(gs[3])
                    if gs[1]:
                        spread(gs[1])

                def restart():
                    dve.wait_ge(L.added, NG)
                    dve.memset(aggT[:], 0.0).then_inc(L.restarted, 1)
                    dve.tensor_scalar(rel_all[:], rel_group[:], float(WN), None, ALU.add).then_inc(L.restarted, 1)
                    dve.tensor_scalar(node_all[:, n, :], node_all[:, n, :], float(-WN), None, ALU.add).then_inc(L.restarted, 1)
                    dve.tensor_scalar(bases[:, n, :], bases[:, n, :], float(-WN), None, ALU.add).then_inc(L.restarted, 1)
                    dve.tensor_copy(place[:].rearrange("p g h -> p (g h)"), node_in_tile.broadcast_to([HW, NG * 2]))\
                       .then_inc(L.restarted, 1)
                    dve.wait_ge(L.restarted, 5)

                def one_pass(k):
                    if not isinstance(k, int):
                        dve.wait_ge(L.added, k * NG)
                        dve.tensor_scalar(rel_all[:], rel_all[:], float(-WN), None, ALU.add).then_inc(L.moved_on, 1)
                        dve.tensor_scalar(node_all[:, n, :], node_all[:, n, :], float(WN), None, ALU.add).then_inc(L.moved_on, 1)
                        dve.tensor_scalar(bases[:, n, :], bases[:, n, :], float(WN), float(NPAD), ALU.add, ALU.min)\
                           .then_inc(L.moved_on, 1)
                        dve.wait_ge(L.moved_on, k * 3)
                    over_steps(dve, k, step, 3)

                dve.wait_ge(agg_cleared[n], 1)
                all_passes(dve, one_pass, restart)

            dve.memset(zero[:], 0.0).then_inc(pad_zero, 1)
            dve.memset(eps[:], EPS).then_inc(eps_set, 1)
            dve.wait_ge(x_in, 16)
            for c in range(NCH):
                layernorm(0, c)
            dve.wait_ge(consts_in, 16)
            dve.wait_ge(windows_in, 16 * 12)
            dve.tensor_tensor(rel_all[:], dst_all, first_all, ALU.subtract).then_inc(windows_set, 1)
            dve.tensor_tensor(rel_group[:], dst_all, group_all, ALU.subtract).then_inc(windows_set, 1)
            dve.tensor_tensor(last_all[:], dst_all, dnext_all, ALU.not_equal).then_inc(windows_set, 1)
            for n in range(2):
                dve.tensor_tensor(node_all[:, n, :], base_all, iota_col.broadcast_to([P, NG]), ALU.add)\
                   .then_inc(windows_set, 1)
            dve.tensor_tensor(place[:], place_all, base_all[0:HW].unsqueeze(2).broadcast_to([HW, NG, 2]), ALU.subtract)\
               .then_inc(place_set, 1)
            dve.wait_ge(place_set, 1)
            dve.tensor_scalar(place[:], place[:], node_in_tile, None, ALU.add).then_inc(windows_set, 1)
            dve.tensor_tensor(tile_row[1].bitcast(F32), tile_row[1], tile_row[0], ALU.subtract).then_inc(span_set, 1)
            dve.tensor_tensor(span, group_row[1], group_row[0], ALU.subtract).then_inc(span_set, 1)
            dve.wait_ge(span_set, 2)
            dve.tensor_reduce(span_max[:, 0:1], tile_row[1].bitcast(F32), AX_X, ALU.max).then_inc(span_max_set, 1)
            dve.tensor_reduce(span_max[:, 1:2], span, AX_X, ALU.max).then_inc(span_max_set, 1)
            dve.wait_ge(span_max_set, 2)
            dve.tensor_scalar(too_wide[:, 0:1], span_max[:, 0:1], float(WN), None, ALU.is_ge).then_inc(wide_set, 1)
            dve.tensor_scalar(too_wide[:, 1:2], span_max[:, 1:2], float(P), None, ALU.is_ge).then_inc(wide_set, 1)
            dve.wait_ge(wide_set, 2)
            dve.tensor_tensor(beyond[:], too_wide[:, 0:1], too_wide[:, 1:2], ALU.max).then_inc(beyond_set, 1)
            dve.tensor_tensor(ident[:], iota_row, iota_col.broadcast_to([P, P]), ALU.is_equal).then_inc(ident_set, 1)
            dve.wait_ge(weights_in, 128)
            dve.tensor_tensor(w0c[:], w0_sb[:], cg_sb[:], ALU.mult).then_inc(w0_set, 1)
            dve.tensor_scalar(relb_sb[:], relT_sb[:], a2b_sb[:, 0:1], None, ALU.add).then_inc(relb_set, 1)
            dve.wait_ge(pw_set, 2)
            dve.tensor_copy(rel_3[:, 0, :], rel_tab[:]).then_inc(rel_3_set, 1)
            dve.wait_ge(rel_3_set, 1)
            dve.tensor_tensor(rel_left[:], rel_tab[:], rel_3[:, 0, :], ALU.subtract).then_inc(rel_left_set, 1)
            dve.wait_ge(rel_left_set, 1)
            dve.tensor_copy(rel_3[:, 1, :], rel_left[:]).then_inc(rel_3_set, 1)
            dve.wait_ge(rel_3_set, 2)
            dve.tensor_tensor(rel_3[:, 2, :], rel_left[:], rel_3[:, 1, :], ALU.subtract).then_inc(rel_3_set, 1)
            dve.wait_ge(windows_set, 6)
            edge_work(0)
            dve.drain().then_inc(sums_done, 1)
            for c in range(NCH + 1):
                if c < NCH:
                    dve.wait_ge(agg_turned, c + 1)
                    xc = X[:, c * MC:(c + 1) * MC, :]
                    dve.tensor_tensor(xc, xc, agg_ps[c % 2], ALU.add).then_inc(agg_used, 1)
                    dve.wait_ge(agg_used, c + 1)
                    layernorm(1, c)
                if c >= 1:
                    split_p(c - 1)
            edge_work(1)
            dve.drain().then_inc(sums_done, 1)
            for c in range(NCH):
                dve.wait_ge(agg_turned, NCH + c + 1)
                xc = X[:, c * MC:(c + 1) * MC, :]
                dve.scalar_tensor_tensor(out=xc, in0=agg_ps[c % 2], scalar=0.0, in1=xc,
                                         op0=ALU.max, op1=ALU.add).then_inc(out_set, 1)


def _cg_table():
    import math
    combos = [(0, 0, 0), (0, 1, 1), (1, 0, 1), (1, 1, 0), (1, 1, 1), (2, 1, 1)]

    def coeff(j1, m1, j2, m2, j3, m3):
        if m3 != m1 + m2:
            return 0.0
        f = math.factorial
        vmin = max(0, j2 - j3 - m1, j1 + m2 - j3)
        vmax = min(j1 + j2 - j3, j1 - m1, j2 + m2)
        pref = (2 * j3 + 1) * f(j3 + j1 - j2) * f(j3 - j1 + j2) * f(j1 + j2 - j3) / f(j1 + j2 + j3 + 1)
        pref *= f(j3 + m3) * f(j3 - m3) * f(j1 - m1) * f(j1 + m1) * f(j2 - m2) * f(j2 + m2)
        total = 0.0
        for v in range(vmin, vmax + 1):
            total += (-1) ** v / (f(v) * f(j1 + j2 - j3 - v) * f(j1 - m1 - v) * f(j2 + m2 - v)
                                  * f(j3 - j2 + m1 + v) * f(j3 - j1 - m2 + v))
        return math.sqrt(pref) * total

    def su2(l1, l2, l3):
        c = np.zeros((2 * l1 + 1, 2 * l2 + 1, 2 * l3 + 1), dtype=np.complex128)
        for m1 in range(-l1, l1 + 1):
            for m2 in range(-l2, l2 + 1):
                if -l3 <= m1 + m2 <= l3:
                    c[m1 + l1, m2 + l2, m1 + m2 + l3] = coeff(l1, m1, l2, m2, l3, m1 + m2)
        return c

    def real(l):
        q = np.zeros((2 * l + 1, 2 * l + 1), dtype=np.complex128)
        for m in range(-l, 0):
            q[l + m, l + abs(m)] = 1 / np.sqrt(2)
            q[l + m, l - abs(m)] = -1j / np.sqrt(2)
        q[l, l] = 1.0
        for m in range(1, l + 1):
            q[l + m, l + abs(m)] = (-1) ** m / np.sqrt(2)
            q[l + m, l - abs(m)] = 1j * (-1) ** m / np.sqrt(2)
        return (-1j) ** l * q

    table = np.zeros((C0, F, F), np.float32)
    which, where_m, where_o = (np.zeros((C0, F, F), np.int64) for _ in range(3))
    feature = {0: lambda m, j: m, 1: lambda m, j: 8 + 3 * m + j}
    first = {0: 0, 1: 1, 2: 4}
    for n, (le, ln, lo) in enumerate(combos):
        cg = np.einsum("ij,kl,mn,ikn->jlm", real(le), real(ln), np.conj(real(lo)).T, su2(le, ln, lo)).real
        cg = cg / np.linalg.norm(cg)
        for (i, j, k), value in np.ndenumerate(cg):
            for m in range(8):
                for o in range(8):
                    at = first[le] + i, feature[ln](m, j), feature[lo](o, k)
                    table[at], which[at], where_m[at], where_o[at] = value, n, m, o
    return table, which, where_m, where_o


def _quarters(w, layer):
    w = np.asarray(w)
    to = np.zeros((4, F, CQ[layer], F), w.dtype)
    for q in range(4):
        lo, hi = QS[layer][q:q + 2]
        to[q, :, 0:hi - lo] = w[lo:hi].transpose(1, 0, 2)
    return to.reshape(P, CQ[layer], F)


def kernel(x, src, dst, edge_attr_3, edge_attr_5, edge_type_86, edge_weight1, L0_gnn_W, L1_gnn_weight, L1_gnn_w_comp,
           L1_gnn_self_loop_weight, L1_gnn_A1_w, L1_gnn_A1_b, L1_gnn_A2_w, L1_gnn_A2_b, L1_gnn_rel_emb):
    import concourse.bacc as _bacc
    from concourse.bass_utils import run_bass_kernel_spmd as _run

    def pad(a, n, value=0):
        a = np.asarray(a)
        return np.concatenate([a, np.full((n - a.shape[0],) + a.shape[1:], value, a.dtype)])

    def turned(a):
        return a.reshape((T, P) + a.shape[1:]).swapaxes(0, 1)

    table, which, where_m, where_o = _cg_table()
    dst = np.asarray(dst)
    dst_pad = pad(dst, EPAD + 1, NOWHERE)
    tile_first = dst[::P]
    group_first = dst[::GE]
    group_of_tile = np.repeat(group_first, J)[:T]
    place_first = np.concatenate([tile_first, group_of_tile[-1:].repeat(NG * J - T)])
    place_first = place_first.reshape(NG, 2, JH).transpose(2, 0, 1).repeat(WN, axis=0)
    steps = np.arange(P, dtype=np.float32)[:, None]
    arrays = {
        "x": pad(x, NPAD),
        "src_t": turned(pad(src, EPAD)),
        "dst_t": turned(dst_pad[:EPAD]),
        "dnext_t": turned(dst_pad[1:]),
        "dst": dst_pad[:EPAD],
        "etype": pad(edge_type_86, EPAD),
        "edge": turned(pad(np.concatenate([np.asarray(edge_weight1), np.asarray(edge_attr_3), np.asarray(edge_attr_5)], axis=1),
                           EPAD)),
        "tile_first": tile_first,
        "tile_last": np.concatenate([dst[P - 1::P], dst[-1:]])[:T],
        "group_first": group_first,
        "group_last": np.concatenate([dst[GE - 1::GE], dst[-1:]])[:NG],
        "group_of_tile": group_of_tile,
        "place_first": place_first,
        "ramp": np.concatenate([np.tile(steps.T, (P, 1)), steps, steps % WN], axis=1),
        "cg": _quarters(table, 0),
        "w0": _quarters(np.asarray(L0_gnn_W)[which, where_m, where_o], 0),
        "w1": _quarters(np.concatenate([np.asarray(L1_gnn_weight), np.asarray(L1_gnn_self_loop_weight)[None]]), 1),
        "a1b": np.concatenate([np.asarray(L1_gnn_A1_w), np.asarray(L1_gnn_A1_b)[:, None]], axis=1),
        "a2": np.asarray(L1_gnn_A2_w),
        "a2b": np.asarray(L1_gnn_A2_b)[:, None],
        "relT": np.asarray(L1_gnn_rel_emb).T,
        "wcomp": np.asarray(L1_gnn_w_comp),
    }
    arrays = {f"in_{k}_dram": np.ascontiguousarray(v) for k, v in arrays.items()}
    nc = _bacc.Bacc("TRN2", target_bir_lowering=False, num_devices=1)
    args = [nc.dram_tensor(k, v.shape, mybir.dt.from_np(v.dtype), kind="ExternalInput").ap() for k, v in arrays.items()]
    args.append(nc.dram_tensor("out_0_dram", (N, F), F32, kind="ExternalOutput").ap())
    build(nc, *args)
    r = _run(nc, [arrays], core_ids=[0])
    return r.results[0]["out_0_dram"]
```

```python
import concourse.bass as bass
from concourse import mybir
from contextlib import ExitStack
import numpy as np

F32 = mybir.dt.float32
I32 = mybir.dt.int32
I16 = mybir.dt.int16
U8 = mybir.dt.uint8
BF16 = mybir.dt.bfloat16
ALU = mybir.AluOpType
ACT = mybir.ActivationFunctionType
AX_X = mybir.AxisListType.X

N, F = 12500, 32
E = 200000
NREL, NBASE = 86, 16
P = 128
M = -(-N // P)
NPAD = M * P
NWIN = NPAD + P
J = 12
GE = P * J
FULL = E // GE
JT = -(-(E - FULL * GE) // P)
NG = FULL + 1
T = FULL * J + JT
EPAD = T * P
WN = 16
JH = J // 2
HW = JH * WN
NCH = 7
MC = M // NCH
MQ = P // F
MU = 3 * MQ
NU = -(-M // MU)
KA = F + 1
KT = KA + NBASE
C0, C1 = 9, 17
PASSES = -(-N // WN)
QS = [[0, 3, 5, 7, 9], [0, 5, 9, 13, 17]]
CQ = [3, 5]
NOWHERE = (1 << 15) - 1
EPS = 1e-5
SUMS0, CENTRED0, SUMS1 = (slice(a * F, (a + 1) * F) for a in range(3))
OUT = [slice(0, 2 * F), SUMS1]
assert N + PASSES * WN + P < NOWHERE and NREL <= 1 << 8
assert NCH * MC == M and FULL % 2 == 0 and JT <= JH


def gathers_of_pass(q):
    return len(range(q, NG, 4)) * J - (J - JT if q == FULL % 4 else 0)


class Group:

    def __init__(self, i, r, k):
        self.i, self.r, self.k = i, r, k
        self.b = r % 2
        self.q = r % 4
        self.s = i * 4 + r
        self.tail = isinstance(self.s, int) and self.s == FULL
        self.nj = JT if self.tail else J

    def order(self):
        return self.k * NG + self.s + 1

    def order2(self):
        return self.k * len(range(self.b, NG, 2)) + self.i * 2 + self.r // 2 + 1

    def order4(self):
        return self.k * len(range(self.q, NG, 4)) + self.i + self.r // 4 + 1

    def halves(self):
        return -(-self.nj // JH), min(self.nj, JH) * WN

    def gathers(self):
        if self.tail:
            return gathers_of_pass(self.q)
        return self.i * J + (self.r // 4 + 1) * J


def unit(u):
    return slice(u * MU, min((u + 1) * MU, M))


def wait(eng, sem, n):
    if not isinstance(n, int) or n > 0:
        eng.wait_ge(sem, n)


def over_steps(eng, k, body, lag):
    def step(i, r):
        body([Group(i, r - d, k) if not isinstance(i, int) or 0 <= i * 4 + r - d < NG else None for d in range(lag + 1)])
    for t in range(4):
        step(0, t)
    with eng.Fori(0, FULL // 4 - 1) as i:
        for u in range(4):
            step(i, 4 + u)
    for t in range(FULL // 4 * 4, NG + lag):
        step(0, t)


def build(nc, x, src_t, dst_t, dnext_t, dst, etype, edge, tile_first, tile_last, group_first, group_last, group_of_tile,
          place_first, ramp, cg, w0, w1, a1b, a2, a2b, relT, wcomp, out):
    h_table = [nc.dram_tensor(f"h_table{n}", (NPAD, F), F32).ap() for n in range(2)]
    dst_short = nc.dram_tensor("dst_short", (EPAD,), I16).ap()
    typ_short = nc.dram_tensor("typ_short", (EPAD,), U8).ap()
    p_table = nc.dram_tensor("p_table", (NWIN, 3 * KA), BF16).ap()

    with ExitStack() as ctx:
        def sb(name, shape, dt=F32):
            return ctx.enter_context(nc.sbuf_tensor(name, shape, dt))

        def sem(name):
            return ctx.enter_context(nc.semaphore(name))

        ps = ctx.enter_context(nc.psum_tensor("ps", [P, 8, 512], F32))
        G_ps = ps[:, 0:2, :]
        ex_ps = ps[:, 2:4, :]
        oT_ps = ps[0:2 * F, 4, :]
        o_ps = ps[0:HW, 5, 0:4 * F].rearrange("p (h o) -> p h o", h=2)
        win_ps = ps[0:3 * F, 6, 0:P]
        agg_ps = [ps[:, b, 0:MC * F].rearrange("p (m f) -> p m f", f=F) for b in range(2)]
        hT_ps = [ps[:, 2 + b, 0:MU // MQ * P] for b in range(2)]
        p_ps = [ps[:, 4 + b, 0:MU * KA] for b in range(2)]

        ramp_sb = sb("ramp_sb", [P, P + 2])
        iota_row, iota_col, node_in_tile = ramp_sb[:, 0:P], ramp_sb[:, P:P + 1], ramp_sb[0:HW, P + 1:P + 2]
        ident = sb("ident", [P, P])
        zero = sb("zero", [P, 3 * KA], BF16)
        eps = sb("eps", [P, 1])
        cg_sb = sb("cg_sb", [P, CQ[0], F])
        w0_sb = sb("w0_sb", [P, CQ[0], F])
        w0c = sb("w0c", [P, CQ[0], 2 * F])
        w0_sum = sb("w0_sum", [P, CQ[0]])
        w1_sb = sb("w1_sb", [P, CQ[1], F])
        a1b_sb = sb("a1b_sb", [F, KA])
        a2_sb = sb("a2_sb", [F, F])
        a2b_sb = sb("a2b_sb", [F, 1])
        relT_sb = sb("relT_sb", [F, NREL])
        relb_sb = sb("relb_sb", [F, NREL])
        p_w4 = sb("p_w4", [P, MQ * KA])
        rel_tab = sb("rel_tab", [NREL, KT])
        rel_left = sb("rel_left", [NREL, KT])
        rel_3 = sb("rel_3", [NREL, 3, KT], BF16)

        X = sb("X", [P, M, F])
        H = sb("H", [P, M, F])
        squares = sb("squares", [P, 2, MC, F])
        row_sum = sb("row_sum", [P, M])
        row_var = sb("row_var", [P, M])
        row_std = sb("row_std", [P, M])
        row_rstd = sb("row_rstd", [P, M])
        hT = sb("hT", [P, 2, MU // MQ * P])
        p_left = sb("p_left", [P, M, KA])
        h0 = p_left[:].rearrange("p m k -> p (m k)")[:, 0:M * F].rearrange("p (m f) -> p m f", f=F)
        h_rows = [h0, H[:]]
        aggT = sb("aggT", [3 * F, NWIN])

        bases = sb("bases", [1, 2, NG], I32)
        node_all = sb("node_all", [P, 2, NG])
        rel_all = sb("rel_all", [P, T])
        rel_group = sb("rel_group", [P, T])
        last_all = sb("last_all", [P, T])
        place = sb("place", [HW, NG, 2])
        span_max = sb("span_max", [1, 2])
        too_wide = sb("too_wide", [1, 2])
        beyond = sb("beyond", [1, 1], I32)

        idx = sb("idx", [P, 2, J], I32)
        coef0 = sb("coef0", [P, 2, J, C0])
        dst_b = sb("dst_b", [P, 2, GE], I16)
        typ_b = sb("typ_b", [NREL, 2, GE], U8)
        p_win = sb("p_win", [P, 2, 3, KA], BF16)
        xg = sb("xg", [P, 4, J, F])
        S = sb("S", [P, 2, J, WN])
        dstT = sb("dstT", [P, J, P], BF16)
        typT = sb("typT", [NREL, J, P], BF16)
        prod = sb("prod", [P, J, F])
        dots = sb("dots", [P, J])
        score = sb("score", [P, J])
        score_r = sb("score_r", [P, J])
        att = sb("att", [P, J])
        coef1 = sb("coef1", [P, 2, J, C1])
        Z = sb("Z", [P, 2, J, C1 * WN])
        R = sb("R", [HW, 2, 2, P])
        G_sb = sb("G_sb", [P, CQ[1], 2, HW])
        oT_sb = sb("oT_sb", [2 * F, 2, HW])
        o_sb = sb("o_sb", [HW, 2, 2 * F])

        room = Z[:].rearrange("p b j z -> p (b j z)").bitcast(I32)
        dst_all, dnext_all, first_all, group_all = (room[:, i * T:(i + 1) * T] for i in range(4))
        scratch = sb("scratch", [P, 5 * NG + 2 * T], I32)
        base_all, place_all = scratch[:, 0:NG], scratch[0:HW, NG:3 * NG].rearrange("p (g h) -> p g h", h=2)
        group_row = [scratch[0:1, (3 + i) * NG:(4 + i) * NG] for i in range(2)]
        tile_row = [scratch[0:1, 5 * NG + i * T:5 * NG + (i + 1) * T] for i in range(2)]
        span = squares[0:1].rearrange("p b m f -> p (b m f)")[:, 0:NG]
        words = p_left[:].rearrange("p m k -> p (m k)").bitcast(I32)
        dst_words, typ_words = words[:, 0:T], words[:, T:2 * T]
        dst_16, typ_8 = scratch[:, 5 * NG:5 * NG + T].bitcast(I16)[:, 0:T], scratch[:, 5 * NG + T:].bitcast(U8)[:, 0:T]
        p_rows = Z[:].rearrange("p b j z -> p (b j z)").bitcast(BF16)[:, 0:M * 3 * KA].rearrange("p (m a k) -> p m a k", a=3, k=KA)

        consts_in, weights_in, windows_in = sem("consts_in"), sem("weights_in"), sem("windows_in")
        x_in = [sem(f"x_in{c}") for c in range(NCH)]
        out_done, pad_done = sem("out_done"), sem("pad_done")
        words_in, short_set, short_stored = sem("words_in"), sem("short_set"), sem("short_stored")
        pad_zero, eps_set = sem("pad_zero"), sem("eps_set")
        ident_set, w0_set, relb_set = sem("ident_set"), sem("w0_set"), sem("relb_set")
        rel_left_set, rel_3_set = sem("rel_left_set"), sem("rel_3_set")
        span_set, span_max_set, wide_set, beyond_set = sem("span_set"), sem("span_max_set"), sem("wide_set"), sem("beyond_set")
        windows_set, place_set = sem("windows_set"), sem("place_set")
        pw_ps_ready, pw_set = sem("pw_ps_ready"), sem("pw_set")
        sum_set, centred_set, squares_set, var_set = sem("sum_set"), sem("centred_set"), sem("squares_set"), sem("var_set")
        std_set, rstd_set, h_set = sem("std_set"), sem("rstd_set"), sem("h_set")
        h_stored = [sem(f"h_stored{n}") for n in range(2)]
        centred_turned, agg_turned = sem("centred_turned"), sem("agg_turned")
        sums_done, x_set, out_set = sem("sums_done"), sem("x_set"), sem("out_set")
        p_w4_zero = sem("p_w4_zero")
        agg_used = sem("agg_used")
        agg_cleared = sem("agg_cleared")
        h_turned, hT_set, p_mm = sem("h_turned"), sem("hT_set"), sem("p_mm")
        p_high_set, p_left_set, p_mid_set, p_set = sem("p_high_set"), sem("p_left_set"), sem("p_mid_set"), sem("p_set")
        p_full_set, p_stored = sem("p_full_set"), sem("p_stored")

        class Edge:

            def __init__(self, n):
                self.idx_in = [sem(f"idx_in{n}_{b}") for b in range(2)]
                self.coef_in = [sem(f"coef_in{n}_{b}") for b in range(2)]
                self.rows_in = [sem(f"rows_in{n}_{b}") for b in range(2)]
                self.pwin_in = [sem(f"pwin_in{n}_{b}") for b in range(2)]
                self.gathered = [sem(f"gathered{n}_{q}") for q in range(4)]
                self.gather_go = sem(f"gather_go{n}")
                self.load_go = sem(f"load_go{n}")
                self.turn_go = sem(f"turn_go{n}")
                self.S_set = sem(f"S_set{n}")
                self.last_set = sem(f"last_set{n}")
                self.dstT_set = sem(f"dstT_set{n}")
                self.typT_set = sem(f"typT_set{n}")
                self.ex_done = sem(f"ex_done{n}")
                self.prod_set = sem(f"prod_set{n}")
                self.dots_set = sem(f"dots_set{n}")
                self.score_set = sem(f"score_set{n}")
                self.score_r_set = sem(f"score_r_set{n}")
                self.att_set = sem(f"att_set{n}")
                self.coef_set = sem(f"coef_set{n}")
                self.Z_set = sem(f"Z_set{n}")
                self.R_set = sem(f"R_set{n}")
                self.summed = sem(f"summed{n}")
                self.G_set = sem(f"G_set{n}")
                self.projected = sem(f"projected{n}")
                self.oT_set = sem(f"oT_set{n}")
                self.turned = sem(f"turned{n}")
                self.o_set = sem(f"o_set{n}")
                self.placed = sem(f"placed{n}")
                self.added = sem(f"added{n}")
                self.restarted = sem(f"restarted{n}")
                self.moved_on = sem(f"moved_on{n}")
                self.recounted = sem(f"recounted{n}")

        layers = [Edge(0), Edge(1)]
        block = ctx.enter_context(nc.Block())

        def all_passes(eng, passes, restart=None, finish=None):
            passes(0)
            eng.wait_ge(beyond_set, 1)
            too_far = eng.value_load(beyond[0:1, 0:1], min_val=0, max_val=1)
            with eng.If(too_far):
                if restart:
                    restart()
                with eng.Fori(1, PASSES + 1) as k:
                    passes(k)
                if finish:
                    finish()

        @block.sync
        def _(sp):
            for c in range(NCH):
                sp.dma_start(X[:, c * MC:(c + 1) * MC, :],
                             x.rearrange("(p m) f -> p m f", m=M)[:, c * MC:(c + 1) * MC, :]).then_inc(x_in[c], 16)
            sp.dma_start(ramp_sb[:], ramp).then_inc(consts_in, 16)
            for to, of in ((dst_all, dst_t), (dnext_all, dnext_t), (first_all, tile_first.partition_broadcast(P)),
                           (group_all, group_of_tile.partition_broadcast(P)), (base_all, group_first.partition_broadcast(P)),
                           (place_all, place_first), (tile_row[0], tile_first.rearrange("(a t) -> a t", a=1)),
                           (tile_row[1], tile_last.rearrange("(a t) -> a t", a=1)),
                           (group_row[0], group_first.rearrange("(a t) -> a t", a=1)),
                           (group_row[1], group_last.rearrange("(a t) -> a t", a=1)),
                           (bases[:, 0, :], group_first.rearrange("(a t) -> a t", a=1)),
                           (bases[:, 1, :], group_first.rearrange("(a t) -> a t", a=1))):
                sp.dma_start(to, of).then_inc(windows_in, 16)
            for to, of in ((cg_sb[:], cg), (w0_sb[:], w0), (w1_sb[:], w1), (a1b_sb[:], a1b), (a2_sb[:], a2), (a2b_sb[:], a2b),
                           (relT_sb[:], relT), (rel_tab[:, KA:KT], wcomp)):
                sp.dma_start(to, of).then_inc(weights_in, 16)
            sp.wait_ge(pad_zero, 1)
            sp.dma_start(p_table[NPAD:NWIN, :], zero[:]).then_inc(pad_done, 16)

            def store_h(n, c):
                table = h_table[n].rearrange("(p m) f -> p m f", m=M)
                sp.wait_ge(h_set, n * NCH + c + 1)
                sp.dma_start(table[:, c * MC:(c + 1) * MC, :], h_rows[n][:, c * MC:(c + 1) * MC, :])\
                  .then_inc(h_stored[n], 16)

            def store_p(u):
                table = p_table[0:NPAD, :].rearrange("(p m) k -> p m k", m=M)
                sp.wait_ge(p_set, u + 1)
                sp.dma_start(table[:, unit(u), :], p_rows[:, unit(u)].rearrange("p m a k -> p m (a k)")).then_inc(p_stored, 16)

            def edge_loads(n):
                L = layers[n]

                def tiles(g):
                    return slice(FULL * J, T) if g.tail else bass.ds(g.s * J, J)

                def load_idx(g):
                    if isinstance(g.s, int) and g.s < 2:
                        if not isinstance(g.k, int):
                            sp.wait_ge(L.added, g.k * NG)
                            sp.nop().then_inc(L.load_go, 1)
                            sp.wait_ge(L.moved_on, g.k * 3)
                            sp.nop().then_inc(L.load_go, 1)
                            sp.wait_ge(L.recounted, g.k)
                            sp.nop().then_inc(L.load_go, 1)
                    else:
                        back = Group(g.i, g.r - 2, g.k)
                        sp.wait_ge(L.gathered[back.q], back.gathers() * 16)
                        sp.nop().then_inc(L.load_go, 1)
                    sp.dma_start(idx[:, g.b, 0:g.nj], src_t[:, tiles(g)]).then_inc(L.idx_in[g.b], 16)

                def load_coefs(g):
                    wait(sp, L.Z_set, g.order() * 2 - 4)
                    sp.nop().then_inc(L.load_go, 1)
                    sp.dma_start(coef0[:, g.b, 0:g.nj, :], edge[:, tiles(g), :]).then_inc(L.coef_in[g.b], 16)

                def load_rows(g):
                    b, ne = g.b, g.nj * P
                    edges = slice(FULL * GE, EPAD) if g.tail else bass.ds(g.s * GE, GE)
                    wait(sp, L.typT_set, g.order() - 2)
                    sp.nop().then_inc(L.load_go, 1)
                    sp.dma_start(dst_b[:, b, 0:ne], dst_short[edges].partition_broadcast(P)).then_inc(L.rows_in[b], 16)
                    sp.dma_start(typ_b[:, b, 0:ne], typ_short[edges].partition_broadcast(NREL)).then_inc(L.rows_in[b], 16)

                def load_pwin(g):
                    base = sp.value_load(bases[0:1, n, bass.ds(g.s, 1)], min_val=0, max_val=NPAD)
                    wait(sp, L.ex_done, g.order() - 2)
                    sp.nop().then_inc(L.load_go, 1)
                    sp.dma_start(p_win[:, g.b].rearrange("p a k -> p (a k)"), p_table[bass.ds(base, P), :])\
                      .then_inc(L.pwin_in[g.b], 16)

                def early(g, groups):
                    return isinstance(g.s, int) and isinstance(g.k, int) and g.s < groups

                def loads(g):
                    if n == 0:
                        load_idx(g)
                        load_coefs(g)
                    else:
                        if not early(g, 3):
                            load_idx(g)
                        if not early(g, 2):
                            load_rows(g)
                        load_pwin(g)

                if n == 1:
                    sp.wait_ge(short_stored, 32)
                    for t in range(2):
                        load_idx(Group(0, t, 0))
                        load_rows(Group(0, t, 0))
                    for u in range(NU):
                        store_p(u)
                    load_idx(Group(0, 2, 0))
                    sp.wait_ge(p_stored, 16 * NU)
                    sp.wait_ge(pad_done, 16)
                all_passes(sp, lambda k: over_steps(sp, k, lambda gs: loads(gs[0]), 0))

            for c in range(NCH):
                store_h(0, c)
            edge_loads(0)
            for c in range(NCH):
                store_h(1, c)
            edge_loads(1)
            left = N - (P - 1) * M
            rows = out[0:(P - 1) * M, :].rearrange("(p m) f -> p m f", m=M)
            rest = out[(P - 1) * M:N, :].rearrange("(a m) f -> a m f", a=1)
            stores = 0
            for c in range(NCH):
                lo, hi = c * MC, (c + 1) * MC
                sp.wait_ge(out_set, c + 1)
                sp.dma_start(rows[0:112, lo:hi, :], X[0:112, lo:hi, :]).then_inc(out_done, 16)
                sp.dma_start(rows[112:P - 1, lo:hi, :], X[112:P - 1, lo:hi, :]).then_inc(out_done, 16)
                stores += 2
                if lo < left:
                    sp.dma_start(rest[:, lo:min(hi, left), :], X[P - 1:P, lo:min(hi, left), :]).then_inc(out_done, 16)
                    stores += 1
            sp.wait_ge(out_done, 16 * stores)

        @block.gpsimd
        def _(pool):
            def edge_gathers(n):
                L = layers[n]

                def gather(g):
                    pool.wait_ge(L.idx_in[g.b], g.order2() * 16)
                    pool.nop().then_inc(L.gather_go, 1)
                    wait(pool, L.summed, g.order() - 4)
                    pool.nop().then_inc(L.gather_go, 1)
                    for j in range(g.nj):
                        pool.indirect_dma_start(
                            xg[:, g.q, j, :], None, h_table[n],
                            bass.IndirectOffsetOnAxis(ap=idx[:, g.b, j:j + 1], axis=0)).then_inc(L.gathered[g.q], 16)

                def one_pass(k):
                    if not isinstance(k, int):
                        pool.wait_ge(L.added, k * NG)
                        pool.nop().then_inc(L.gather_go, 1)
                        pool.inc_swdge_sem(L.gathered, [16 * gathers_of_pass(q) for q in range(4)], mode="sub")
                        pool.nop().then_inc(L.recounted, 1)
                    over_steps(pool, k, lambda gs: gather(gs[0]), 0)

                all_passes(pool, one_pass)

            pool.memset(aggT[:], 0.0).then_inc(agg_cleared, 1)
            for n in range(2):
                pool.wait_ge(h_stored[n], 16 * NCH)
                edge_gathers(n)

        @block.tensor
        def _(pe):
            def turn_agg(rows, c, used, count, done):
                wait(pe, used, count)
                for m in range(MC):
                    at = c * MC + m
                    last = pe.transpose(agg_ps[c % 2][:, m, :], aggT[rows, at:at + M * (P - 1) + 1:M], ident[rows, rows])
                last.then_inc(done, 1)

            def node_tables(u):
                if u < NU:
                    pe.wait_ge(h_set, NCH + -(-unit(u).stop // MC))
                    wait(pe, hT_set, u - 1)
                    for m in range(0, unit(u).stop - u * MU, MQ):
                        four = H[:, u * MU + m:min(u * MU + m + MQ, M), :].rearrange("p m f -> p (m f)")
                        last = pe.transpose(hT_ps[u % 2][0:four.shape[1], m * F:m * F + P], four, ident[:])
                    last.then_inc(h_turned, 1)
                if u >= 1:
                    v = u - 1
                    pe.wait_ge(hT_set, v + 1)
                    wait(pe, p_high_set, v - 1)
                    for m in range(0, unit(v).stop - v * MU, MQ):
                        k = min(MQ, M - v * MU - m)
                        last = pe.matmul(p_ps[v % 2][:, m * KA:(m + k) * KA], hT[0:k * F, v % 2, m * F:m * F + P],
                                         p_w4[0:k * F, 0:k * KA], start=True, stop=True)
                    last.then_inc(p_mm, 1)

            def edge_sums(n):
                L = layers[n]
                qs, cq = QS[n], CQ[n]
                no = OUT[n].stop - OUT[n].start
                weights = w0c if n == 0 else w1_sb

                def attention_rows(g):
                    pe.wait_ge(L.typT_set, g.order())
                    pe.wait_ge(L.pwin_in[g.b], g.order2() * 16)
                    wait(pe, L.coef_set, g.order() - 1)
                    for j in range(g.nj):
                        to = ex_ps[:, j // JH, j % JH * KT:j % JH * KT + KT]
                        for a in range(3):
                            pe.matmul(to, typT[:, j, :], rel_3[:, a, :], start=(a == 0), stop=False)
                        for a in range(3):
                            last = pe.matmul(to[:, 0:KA], dstT[:, j, :], p_win[:, g.b, a, :], start=False, stop=(a == 2))
                    last.then_inc(L.ex_done, 1)

                def project(g):
                    hh, w = g.halves()
                    pe.wait_ge(L.G_set, g.order())
                    wait(pe, L.oT_set, g.order() - 1)
                    for c in range(cq):
                        rows = P if c < cq - 1 else F
                        last = pe.matmul(oT_ps[0:no, 0:hh * w], weights[0:rows, c, :], G_sb[0:rows, c, 0:hh, 0:w],
                                         start=(c == 0), stop=(c == cq - 1))
                    last.then_inc(L.projected, 1)

                def turn(g):
                    hh, w = g.halves()
                    pe.wait_ge(L.oT_set, g.order())
                    wait(pe, L.o_set, g.order() - 1)
                    pe.nop().then_inc(L.turn_go, 1)
                    for h in range(hh):
                        last = pe.transpose(o_ps[0:w, h, 0:no], oT_sb[0:no, h, 0:w], ident[0:no, 0:no])
                    last.then_inc(L.turned, 1)

                def place_rows(g):
                    hh, w = g.halves()
                    pe.wait_ge(L.o_set, g.order())
                    pe.wait_ge(L.R_set, g.order())
                    wait(pe, L.added, g.order() - 1)
                    pe.nop().then_inc(L.turn_go, 1)
                    for h in range(hh):
                        last = pe.matmul(win_ps[OUT[n]], o_sb[0:w, h, 0:no], R[0:w, g.b, h, :], start=(h == 0),
                                         stop=(h == hh - 1), tile_position=(0, OUT[n].start))
                    last.then_inc(L.placed, 1)

                def sum_edges(g, back):
                    wait(pe, L.G_set, g.order() - 1)
                    pe.wait_ge(L.gathered[g.q], g.gathers() * 16)
                    pe.wait_ge(L.Z_set, g.order() * 2 - 1)
                    for j in range(g.nj):
                        if j == JH:
                            pe.wait_ge(L.Z_set, g.order() * 2)
                        bank = G_ps[:, j // JH, 0:cq * HW].rearrange("p (c j n) -> p c j n", c=cq, j=JH)
                        for q in range(4):
                            last = pe.matmul(bank[q * F:(q + 1) * F, 0:qs[q + 1] - qs[q], j % JH, :], xg[:, g.q, j, :],
                                             Z[:, g.b, j, qs[q] * WN:qs[q + 1] * WN], start=True, stop=True,
                                             tile_position=(0, q * F))
                        if j == g.nj - 1:
                            last.then_inc(L.summed, 1)
                        if back and j == min(g.nj, J // 3) - 1:
                            turn(back)
                        if back and j == min(g.nj, 2 * J // 3) - 1:
                            place_rows(back)

                def step(gs):
                    if n == 1 and gs[0]:
                        attention_rows(gs[0])
                    if gs[2]:
                        project(gs[2])
                    if gs[1]:
                        sum_edges(gs[1], gs[2])
                    elif gs[2]:
                        turn(gs[2])
                        place_rows(gs[2])

                def one_pass(k):
                    if not isinstance(k, int):
                        pe.wait_ge(L.recounted, k)
                    over_steps(pe, k, step, 2)

                all_passes(pe, one_pass)

            pe.wait_ge(weights_in, 128)
            pe.wait_ge(relb_set, 1)
            for q in range(MQ):
                pe.matmul(ps[q * F:(q + 1) * F, 6, 0:KA], a2_sb[:], a1b_sb[:], start=True, stop=True, tile_position=(0, q * F))
            pe.matmul(ps[0:NREL, 7, 0:KA], relb_sb[:], a1b_sb[:], start=True, stop=True).then_inc(pw_ps_ready, 1)
            pe.wait_ge(ident_set, 1)
            pe.wait_ge(w0_set, 3)
            pe.wait_ge(pw_set, 1 + MQ)
            edge_sums(0)
            pe.wait_ge(sums_done, 1)
            for c in range(NCH):
                turn_agg(CENTRED0, c, agg_used, c - 1, centred_turned)
            for u in range(NU + 1):
                node_tables(u)
            pe.wait_ge(agg_used, NCH)
            for c in range(NCH):
                turn_agg(SUMS0, c, x_set, c - 1, agg_turned)
            pe.wait_ge(p_high_set, NU)
            pe.wait_ge(x_set, NCH)
            pe.wait_ge(rel_3_set, 3)
            edge_sums(1)
            pe.wait_ge(sums_done, 2)
            for c in range(NCH):
                turn_agg(SUMS1, c, out_set, c - 1, agg_turned)

        @block.scalar
        def _(act):
            def node_rows(n, c):
                if c < NCH:
                    act.wait_ge(agg_used if n else centred_set, c + 1)
                    if c >= 2:
                        act.wait_ge(var_set, n * NCH + c - 1)
                    act.activation(squares[:, c % 2], H[:, c * MC:(c + 1) * MC, :], ACT.Square).then_inc(squares_set, 1)
                if c >= 1:
                    act.wait_ge(var_set, n * NCH + c)
                    act.activation(row_std[:, (c - 1) * MC:c * MC], row_var[:, (c - 1) * MC:c * MC], ACT.Sqrt,
                                   bias=eps[:, 0:1], scale=1.0 / F).then_inc(std_set, 1)

            def node_tables(u):
                if u < NU:
                    act.wait_ge(h_turned, u + 1)
                    wait(act, p_mm, u - 1)
                    k, n = min(MQ, M - u * MU) * F, -(-(unit(u).stop - u * MU) // MQ) * P
                    act.activation(hT[0:k, u % 2, 0:n], hT_ps[u % 2][0:k, 0:n], ACT.Copy).then_inc(hT_set, 1)
                if u >= 1:
                    v = u - 1
                    act.wait_ge(p_mm, v + 1)
                    rows = p_ps[v % 2][:, 0:(unit(v).stop - v * MU) * KA].rearrange("p (m k) -> p m k", k=KA)
                    act.activation(p_left[:, unit(v), :], rows, ACT.Copy).then_inc(p_full_set, 1)
                    act.activation(p_rows[:, unit(v), 0, :], rows, ACT.Copy).then_inc(p_high_set, 1)

            def edge_copies(n):
                L = layers[n]
                cq = CQ[n]
                no = OUT[n].stop - OUT[n].start

                def attention(g):
                    act.wait_ge(L.score_set, g.order())
                    act.activation(score_r[:, 0:g.nj], score[:, 0:g.nj], ACT.Relu).then_inc(L.score_r_set, 1)
                    act.wait_ge(L.score_r_set, g.order())
                    act.activation(att[:, 0:g.nj], score_r[:, 0:g.nj], ACT.Tanh, scale=float(F) ** -0.5)\
                       .then_inc(L.att_set, 1)

                def copy_G(g):
                    hh, w = g.halves()
                    act.wait_ge(L.summed, g.order())
                    wait(act, L.projected, g.order() - 1)
                    bank = G_ps[:, 0:hh, 0:cq * HW].rearrange("p h (c w) -> p h c w", c=cq)
                    to = G_sb[:, 0:cq, 0:hh, 0:w].rearrange("p c h w -> p h c w")
                    act.activation(to[0:F, :, cq - 1, :], bank[0:F, :, cq - 1, 0:w], ACT.Copy)
                    act.activation(to[:, :, 0:cq - 1, :], bank[:, :, 0:cq - 1, 0:w], ACT.Copy).then_inc(L.G_set, 1)

                def copy_oT(g):
                    hh, w = g.halves()
                    act.wait_ge(L.projected, g.order())
                    wait(act, L.turned, g.order() - 1)
                    act.activation(oT_sb[0:no, 0:hh, 0:w], oT_ps[0:no, 0:hh * w].rearrange("p (h w) -> p h w", h=hh),
                                   ACT.Copy).then_inc(L.oT_set, 1)

                def copy_o(g):
                    hh, w = g.halves()
                    act.wait_ge(L.turned, g.order())
                    wait(act, L.placed, g.order() - 1)
                    act.activation(o_sb[0:w, 0:hh, 0:no], o_ps[0:w, 0:hh, 0:no], ACT.Copy).then_inc(L.o_set, 1)

                def step(gs):
                    if n == 1 and gs[1]:
                        attention(gs[1])
                    if gs[2]:
                        copy_G(gs[2])
                        copy_oT(gs[2])
                        copy_o(gs[2])

                all_passes(act, lambda k: over_steps(act, k, step, 2))

            act.wait_ge(eps_set, 1)
            act.activation(row_std[:, 0:1], eps[:], ACT.Sqrt)
            for c in range(NCH + 1):
                node_rows(0, c)
            act.wait_ge(h_stored[0], 16 * NCH)
            act.dma_start(dst_words, dst.rearrange("(p t) -> p t", t=T)).then_inc(words_in, 16)
            act.dma_start(typ_words, etype.rearrange("(p t) -> p t", t=T)).then_inc(words_in, 16)
            act.wait_ge(pw_ps_ready, 1)
            act.wait_ge(p_w4_zero, 1)
            for q in range(MQ):
                at = slice(q * F, (q + 1) * F)
                act.activation(p_w4[at, q * KA:(q + 1) * KA], ps[at, 6, 0:KA], ACT.Copy).then_inc(pw_set, 1)
            act.activation(rel_tab[:, 0:KA], ps[0:NREL, 7, 0:KA], ACT.Copy).then_inc(pw_set, 1)
            act.wait_ge(short_set, 2)
            act.dma_start(dst_short.rearrange("(p t) -> p t", t=T), dst_16).then_inc(short_stored, 16)
            act.dma_start(typ_short.rearrange("(p t) -> p t", t=T), typ_8).then_inc(short_stored, 16)
            edge_copies(0)
            for c in range(NCH + 1):
                node_rows(1, c)
            for u in range(NU + 1):
                node_tables(u)
            edge_copies(1)

        @block.vector
        def _(dve):
            def node_rows(n):
                for c in range(NCH + 2):
                    new, mid, old = (slice(a * MC, (a + 1) * MC) for a in (c, c - 1, c - 2))
                    o = n * NCH + c + 1
                    if n == 1 and c < NCH:
                        dve.wait_ge(centred_turned, c + 1)
                        dve.tensor_tensor(H[:, new, :], H[:, new, :], agg_ps[c % 2], ALU.add).then_inc(agg_used, 1)
                    if 1 <= c <= NCH:
                        dve.wait_ge(squares_set, o - 1)
                        dve.tensor_reduce(row_var[:, mid], squares[:, (c - 1) % 2], AX_X, ALU.add).then_inc(var_set, 1)
                    if n == 0 and c < NCH:
                        dve.wait_ge(x_in[c], 16)
                        dve.tensor_reduce(row_sum[:, new], X[:, new, :], AX_X, ALU.add).then_inc(sum_set, 1)
                    if c >= 2:
                        dve.wait_ge(std_set, o - 2)
                        dve.reciprocal(row_rstd[:, old], row_std[:, old]).then_inc(rstd_set, 1)
                    if n == 0 and c < NCH:
                        dve.wait_ge(sum_set, o)
                        dve.scalar_tensor_tensor(out=H[:, new, :], in0=row_sum[:, new].unsqueeze(2).broadcast_to([P, MC, F]),
                                                 scalar=-1.0 / F, in1=X[:, new, :], op0=ALU.mult, op1=ALU.add)\
                           .then_inc(centred_set, 1)
                    if c >= 2:
                        dve.wait_ge(rstd_set, o - 2)
                        dve.wait_ge(squares_set, o - 2)
                        dve.scalar_tensor_tensor(out=h_rows[n][:, old, :], in0=H[:, old, :], scalar=0.0,
                                                 in1=row_rstd[:, old].unsqueeze(2).broadcast_to([P, MC, F]),
                                                 op0=ALU.max, op1=ALU.mult).then_inc(h_set, 1)

            def split_p(c):
                at = unit(c)
                dve.wait_ge(p_high_set, c + 1)
                dve.tensor_tensor(p_left[:, at, :], p_left[:, at, :], p_rows[:, at, 0, :], ALU.subtract).then_inc(p_left_set, 1)
                dve.wait_ge(p_left_set, c + 1)
                dve.tensor_copy(p_rows[:, at, 1, :], p_left[:, at, :]).then_inc(p_mid_set, 1)
                dve.wait_ge(p_mid_set, c + 1)
                dve.tensor_tensor(p_rows[:, at, 2, :], p_left[:, at, :], p_rows[:, at, 1, :], ALU.subtract).then_inc(p_set, 1)

            def edge_work(n):
                L = layers[n]
                C = C0 if n == 0 else C1

                def tiles(v, g):
                    return v[:, FULL * J:T] if g.tail else v[:, bass.ds(g.s * J, J)]

                def one_hots(g):
                    b, nj, o = g.b, g.nj, g.order()
                    wait(dve, L.Z_set, o * 2 - 4)
                    dve.tensor_tensor(S[:, b, 0:nj, :], tiles(rel_all, g).unsqueeze(2).broadcast_to([P, nj, WN]),
                                      iota_row[:, 0:WN].unsqueeze(1).broadcast_to([P, nj, WN]), ALU.is_equal)\
                       .then_inc(L.S_set, 1)
                    if n == 1:
                        dve.tensor_copy(coef1[:, b, 0:nj, NBASE], tiles(last_all, g)).then_inc(L.last_set, 1)
                        dve.wait_ge(L.rows_in[b], g.order2() * 32)
                        wait(dve, L.ex_done, o - 1)
                        node = node_all[:, n, FULL:NG] if g.tail else node_all[:, n, bass.ds(g.s, 1)]
                        dve.tensor_scalar(dstT[:, 0:nj, :].rearrange("p j e -> p (j e)"), dst_b[:, b, 0:nj * P], node, None,
                                          ALU.is_equal).then_inc(L.dstT_set, 1)
                        dve.wait_ge(L.dstT_set, o)
                        dve.tensor_scalar(typT[:, 0:nj, :].rearrange("p j e -> p (j e)"), typ_b[:, b, 0:nj * P],
                                          iota_col[0:NREL], None, ALU.is_equal).then_inc(L.typT_set, 1)

                def banks(v, nj):
                    return v.rearrange("p (h j) f -> p h j f", j=min(nj, JH))

                def ex_rows(nj):
                    return ex_ps[:, 0:-(-nj // JH), 0:min(nj, JH) * KT].rearrange("p h (j k) -> p h j k", k=KT)

                def scores(g):
                    nj, o = g.nj, g.order()
                    rows = ex_rows(nj)
                    dve.wait_ge(L.gathered[g.q], g.gathers() * 16)
                    dve.wait_ge(L.ex_done, o)
                    dve.tensor_tensor(banks(prod[:, 0:nj, :], nj), banks(xg[:, g.q, 0:nj, :], nj), rows[:, :, :, 0:F],
                                      ALU.mult).then_inc(L.prod_set, 1)
                    dve.wait_ge(L.prod_set, o)
                    dve.tensor_reduce(dots[:, 0:nj], prod[:, 0:nj, :], AX_X, ALU.add).then_inc(L.dots_set, 1)
                    dve.wait_ge(L.dots_set, o)
                    two, jj = "p (h j) -> p h j", min(nj, JH)
                    dve.tensor_tensor(score[:, 0:nj].rearrange(two, j=jj), dots[:, 0:nj].rearrange(two, j=jj),
                                      rows[:, :, :, F], ALU.add).then_inc(L.score_set, 1)

                def coefficients(g):
                    nj = g.nj
                    dve.wait_ge(L.att_set, g.order())
                    dve.tensor_tensor(banks(coef1[:, g.b, 0:nj, 0:NBASE], nj), ex_rows(nj)[:, :, :, KA:KT],
                                      banks(att[:, 0:nj].unsqueeze(2).broadcast_to([P, nj, NBASE]), nj),
                                      ALU.mult).then_inc(L.coef_set, 1)

                def spread(g):
                    b, nj, o = g.b, g.nj, g.order()
                    if n == 0:
                        dve.wait_ge(L.coef_in[b], g.order2() * 16)
                        coef = coef0[:, b, 0:nj, :]
                    else:
                        dve.wait_ge(L.coef_set, o)
                        dve.wait_ge(L.last_set, o)
                        coef = coef1[:, b, 0:nj, :]
                    dve.wait_ge(L.S_set, o)
                    wait(dve, L.summed, o - 2)
                    for lo in range(0, nj, JH):
                        js, k = slice(lo, min(lo + JH, nj)), min(JH, nj - lo)
                        dve.tensor_tensor(Z[:, b, js, 0:C * WN].rearrange("p j (c n) -> p j c n", n=WN),
                                          coef[:, js, :].unsqueeze(3).broadcast_to([P, k, C, WN]),
                                          S[:, b, js, :].unsqueeze(2).broadcast_to([P, k, C, WN]),
                                          ALU.mult).then_inc(L.Z_set, 2 if g.tail else 1)
                    hh, w = g.halves()
                    wait(dve, L.placed, o - 2)
                    at = place[0:w, FULL, 0:hh] if g.tail else place[0:w, bass.ds(g.s, 1), :].rearrange("p a h -> p (a h)")
                    dve.tensor_tensor(R[0:w, b, 0:hh, :], at.unsqueeze(2).broadcast_to([w, hh, P]),
                                      iota_row[0:w].unsqueeze(1).broadcast_to([w, hh, P]), ALU.is_equal)\
                       .then_inc(L.R_set, 1)

                def add(g):
                    base = dve.value_load(bases[0:1, n, bass.ds(g.s, 1)], min_val=0, max_val=NPAD)
                    dve.wait_ge(L.placed, g.order())
                    wait(dve, L.added, g.order() - 1)
                    window = aggT[OUT[n], bass.ds(base, P)]
                    dve.tensor_tensor(window, window, win_ps[OUT[n]], ALU.add).then_inc(L.added, 1)

                def step(gs):
                    if n == 1 and gs[1]:
                        scores(gs[1])
                    if gs[0]:
                        one_hots(gs[0])
                    if n == 1 and gs[1]:
                        coefficients(gs[1])
                    if gs[3]:
                        add(gs[3])
                    if gs[1]:
                        spread(gs[1])

                def restart():
                    dve.wait_ge(L.added, NG)
                    dve.memset(aggT[OUT[n], :], 0.0).then_inc(L.restarted, 1)
                    dve.tensor_scalar(rel_all[:], rel_group[:], float(WN), None, ALU.add).then_inc(L.restarted, 1)
                    dve.tensor_scalar(node_all[:, n, :], node_all[:, n, :], float(-WN), None, ALU.add).then_inc(L.restarted, 1)
                    dve.tensor_scalar(bases[:, n, :], bases[:, n, :], float(-WN), None, ALU.add).then_inc(L.restarted, 1)
                    dve.tensor_copy(place[:].rearrange("p g h -> p (g h)"), node_in_tile.broadcast_to([HW, NG * 2]))\
                       .then_inc(L.restarted, 1)
                    dve.wait_ge(L.restarted, 5)

                def one_pass(k):
                    if not isinstance(k, int):
                        dve.wait_ge(L.added, k * NG)
                        dve.tensor_scalar(rel_all[:], rel_all[:], float(-WN), None, ALU.add).then_inc(L.moved_on, 1)
                        dve.tensor_scalar(node_all[:, n, :], node_all[:, n, :], float(WN), None, ALU.add).then_inc(L.moved_on, 1)
                        dve.tensor_scalar(bases[:, n, :], bases[:, n, :], float(WN), float(NPAD), ALU.add, ALU.min)\
                           .then_inc(L.moved_on, 1)
                        dve.wait_ge(L.moved_on, k * 3)
                        dve.wait_ge(L.recounted, k)
                    over_steps(dve, k, step, 3)

                dve.wait_ge(agg_cleared, 1)
                all_passes(dve, one_pass, restart, lambda: dve.wait_ge(L.added, (PASSES + 1) * NG))
                dve.wait_ge(L.added, NG)
                dve.nop().then_inc(sums_done, 1)

            dve.memset(zero[:], 0.0).then_inc(pad_zero, 1)
            dve.memset(eps[:], EPS).then_inc(eps_set, 1)
            dve.memset(p_w4[:], 0.0).then_inc(p_w4_zero, 1)
            node_rows(0)
            dve.wait_ge(consts_in, 16)
            dve.wait_ge(windows_in, 16 * 12)
            dve.tensor_tensor(rel_all[:], dst_all, first_all, ALU.subtract).then_inc(windows_set, 1)
            dve.tensor_tensor(rel_group[:], dst_all, group_all, ALU.subtract).then_inc(windows_set, 1)
            dve.tensor_tensor(last_all[:], dst_all, dnext_all, ALU.not_equal).then_inc(windows_set, 1)
            for n in range(2):
                dve.tensor_tensor(node_all[:, n, :], base_all, iota_col.broadcast_to([P, NG]), ALU.add)\
                   .then_inc(windows_set, 1)
            dve.tensor_tensor(place[:], place_all, base_all[0:HW].unsqueeze(2).broadcast_to([HW, NG, 2]), ALU.subtract)\
               .then_inc(place_set, 1)
            dve.wait_ge(place_set, 1)
            dve.tensor_scalar(place[:], place[:], node_in_tile, None, ALU.add).then_inc(windows_set, 1)
            dve.tensor_tensor(tile_row[1].bitcast(F32), tile_row[1], tile_row[0], ALU.subtract).then_inc(span_set, 1)
            dve.tensor_tensor(span, group_row[1], group_row[0], ALU.subtract).then_inc(span_set, 1)
            dve.wait_ge(span_set, 2)
            dve.tensor_reduce(span_max[:, 0:1], tile_row[1].bitcast(F32), AX_X, ALU.max).then_inc(span_max_set, 1)
            dve.tensor_reduce(span_max[:, 1:2], span, AX_X, ALU.max).then_inc(span_max_set, 1)
            dve.wait_ge(span_max_set, 2)
            dve.tensor_scalar(too_wide[:, 0:1], span_max[:, 0:1], float(WN), None, ALU.is_ge).then_inc(wide_set, 1)
            dve.tensor_scalar(too_wide[:, 1:2], span_max[:, 1:2], float(P), None, ALU.is_ge).then_inc(wide_set, 1)
            dve.wait_ge(wide_set, 2)
            dve.tensor_tensor(beyond[:], too_wide[:, 0:1], too_wide[:, 1:2], ALU.max).then_inc(beyond_set, 1)
            dve.tensor_tensor(ident[:], iota_row, iota_col.broadcast_to([P, P]), ALU.is_equal).then_inc(ident_set, 1)
            dve.wait_ge(weights_in, 128)
            dve.tensor_tensor(w0c[:, :, 0:F], w0_sb[:], cg_sb[:], ALU.mult).then_inc(w0_set, 1)
            dve.wait_ge(w0_set, 1)
            dve.tensor_reduce(w0_sum[:], w0c[:, :, 0:F], AX_X, ALU.add).then_inc(w0_set, 1)
            dve.wait_ge(w0_set, 2)
            dve.scalar_tensor_tensor(out=w0c[:, :, F:2 * F], in0=w0_sum[:].unsqueeze(2).broadcast_to([P, CQ[0], F]),
                                     scalar=-1.0 / F, in1=w0c[:, :, 0:F], op0=ALU.mult, op1=ALU.add).then_inc(w0_set, 1)
            dve.tensor_scalar(relb_sb[:], relT_sb[:], a2b_sb[:, 0:1], None, ALU.add).then_inc(relb_set, 1)
            dve.wait_ge(pw_set, 1 + MQ)
            dve.tensor_copy(rel_3[:, 0, :], rel_tab[:]).then_inc(rel_3_set, 1)
            dve.wait_ge(rel_3_set, 1)
            dve.tensor_tensor(rel_left[:], rel_tab[:], rel_3[:, 0, :], ALU.subtract).then_inc(rel_left_set, 1)
            dve.wait_ge(rel_left_set, 1)
            dve.tensor_copy(rel_3[:, 1, :], rel_left[:]).then_inc(rel_3_set, 1)
            dve.wait_ge(rel_3_set, 2)
            dve.tensor_tensor(rel_3[:, 2, :], rel_left[:], rel_3[:, 1, :], ALU.subtract).then_inc(rel_3_set, 1)
            dve.wait_ge(words_in, 32)
            dve.tensor_copy(dst_16, dst_words).then_inc(short_set, 1)
            dve.tensor_copy(typ_8, typ_words).then_inc(short_set, 1)
            dve.wait_ge(windows_set, 6)
            edge_work(0)
            dve.wait_ge(h_stored[0], 16 * NCH)
            node_rows(1)
            for u in range(NU):
                split_p(u)
            for c in range(NCH):
                dve.wait_ge(agg_turned, c + 1)
                xc = X[:, c * MC:(c + 1) * MC, :]
                dve.tensor_tensor(xc, xc, agg_ps[c % 2], ALU.add).then_inc(x_set, 1)
            edge_work(1)
            for c in range(NCH):
                dve.wait_ge(agg_turned, NCH + c + 1)
                xc = X[:, c * MC:(c + 1) * MC, :]
                dve.scalar_tensor_tensor(out=xc, in0=agg_ps[c % 2], scalar=0.0, in1=xc,
                                         op0=ALU.max, op1=ALU.add).then_inc(out_set, 1)


def _cg_table():
    import math
    combos = [(0, 0, 0), (0, 1, 1), (1, 0, 1), (1, 1, 0), (1, 1, 1), (2, 1, 1)]

    def coeff(j1, m1, j2, m2, j3, m3):
        if m3 != m1 + m2:
            return 0.0
        f = math.factorial
        vmin = max(0, j2 - j3 - m1, j1 + m2 - j3)
        vmax = min(j1 + j2 - j3, j1 - m1, j2 + m2)
        pref = (2 * j3 + 1) * f(j3 + j1 - j2) * f(j3 - j1 + j2) * f(j1 + j2 - j3) / f(j1 + j2 + j3 + 1)
        pref *= f(j3 + m3) * f(j3 - m3) * f(j1 - m1) * f(j1 + m1) * f(j2 - m2) * f(j2 + m2)
        total = 0.0
        for v in range(vmin, vmax + 1):
            total += (-1) ** v / (f(v) * f(j1 + j2 - j3 - v) * f(j1 - m1 - v) * f(j2 + m2 - v)
                                  * f(j3 - j2 + m1 + v) * f(j3 - j1 - m2 + v))
        return math.sqrt(pref) * total

    def su2(l1, l2, l3):
        c = np.zeros((2 * l1 + 1, 2 * l2 + 1, 2 * l3 + 1), dtype=np.complex128)
        for m1 in range(-l1, l1 + 1):
            for m2 in range(-l2, l2 + 1):
                if -l3 <= m1 + m2 <= l3:
                    c[m1 + l1, m2 + l2, m1 + m2 + l3] = coeff(l1, m1, l2, m2, l3, m1 + m2)
        return c

    def real(l):
        q = np.zeros((2 * l + 1, 2 * l + 1), dtype=np.complex128)
        for m in range(-l, 0):
            q[l + m, l + abs(m)] = 1 / np.sqrt(2)
            q[l + m, l - abs(m)] = -1j / np.sqrt(2)
        q[l, l] = 1.0
        for m in range(1, l + 1):
            q[l + m, l + abs(m)] = (-1) ** m / np.sqrt(2)
            q[l + m, l - abs(m)] = 1j * (-1) ** m / np.sqrt(2)
        return (-1j) ** l * q

    table = np.zeros((C0, F, F), np.float32)
    which, where_m, where_o = (np.zeros((C0, F, F), np.int64) for _ in range(3))
    feature = {0: lambda m, j: m, 1: lambda m, j: 8 + 3 * m + j}
    first = {0: 0, 1: 1, 2: 4}
    for n, (le, ln, lo) in enumerate(combos):
        cg = np.einsum("ij,kl,mn,ikn->jlm", real(le), real(ln), np.conj(real(lo)).T, su2(le, ln, lo)).real
        cg = cg / np.linalg.norm(cg)
        for (i, j, k), value in np.ndenumerate(cg):
            for m in range(8):
                for o in range(8):
                    at = first[le] + i, feature[ln](m, j), feature[lo](o, k)
                    table[at], which[at], where_m[at], where_o[at] = value, n, m, o
    return table, which, where_m, where_o


def _quarters(w, layer):
    w = np.asarray(w)
    to = np.zeros((4, F, CQ[layer], F), w.dtype)
    for q in range(4):
        lo, hi = QS[layer][q:q + 2]
        to[q, :, 0:hi - lo] = w[lo:hi].transpose(1, 0, 2)
    return to.reshape(P, CQ[layer], F)


def kernel(x, src, dst, edge_attr_3, edge_attr_5, edge_type_86, edge_weight1, L0_gnn_W, L1_gnn_weight, L1_gnn_w_comp,
           L1_gnn_self_loop_weight, L1_gnn_A1_w, L1_gnn_A1_b, L1_gnn_A2_w, L1_gnn_A2_b, L1_gnn_rel_emb):
    import concourse.bacc as _bacc
    from concourse.bass_utils import run_bass_kernel_spmd as _run

    def pad(a, n, value=0):
        a = np.asarray(a)
        return np.concatenate([a, np.full((n - a.shape[0],) + a.shape[1:], value, a.dtype)])

    def turned(a):
        return a.reshape((T, P) + a.shape[1:]).swapaxes(0, 1)

    table, which, where_m, where_o = _cg_table()
    dst = np.asarray(dst)
    dst_pad = pad(dst, EPAD + 1, NOWHERE)
    tile_first = dst[::P]
    group_first = dst[::GE]
    group_of_tile = np.repeat(group_first, J)[:T]
    place_first = np.concatenate([tile_first, group_of_tile[-1:].repeat(NG * J - T)])
    place_first = place_first.reshape(NG, 2, JH).transpose(2, 0, 1).repeat(WN, axis=0)
    steps = np.arange(P, dtype=np.float32)[:, None]
    arrays = {
        "x": pad(x, NPAD),
        "src_t": turned(pad(src, EPAD)),
        "dst_t": turned(dst_pad[:EPAD]),
        "dnext_t": turned(dst_pad[1:]),
        "dst": dst_pad[:EPAD],
        "etype": pad(edge_type_86, EPAD),
        "edge": turned(pad(np.concatenate([np.asarray(edge_weight1), np.asarray(edge_attr_3), np.asarray(edge_attr_5)], axis=1),
                           EPAD)),
        "tile_first": tile_first,
        "tile_last": np.concatenate([dst[P - 1::P], dst[-1:]])[:T],
        "group_first": group_first,
        "group_last": np.concatenate([dst[GE - 1::GE], dst[-1:]])[:NG],
        "group_of_tile": group_of_tile,
        "place_first": place_first,
        "ramp": np.concatenate([np.tile(steps.T, (P, 1)), steps, steps % WN], axis=1),
        "cg": _quarters(table, 0),
        "w0": _quarters(np.asarray(L0_gnn_W)[which, where_m, where_o], 0),
        "w1": _quarters(np.concatenate([np.asarray(L1_gnn_weight), np.asarray(L1_gnn_self_loop_weight)[None]]), 1),
        "a1b": np.concatenate([np.asarray(L1_gnn_A1_w), np.asarray(L1_gnn_A1_b)[:, None]], axis=1),
        "a2": np.asarray(L1_gnn_A2_w),
        "a2b": np.asarray(L1_gnn_A2_b)[:, None],
        "relT": np.asarray(L1_gnn_rel_emb).T,
        "wcomp": np.asarray(L1_gnn_w_comp),
    }
    arrays = {f"in_{k}_dram": np.ascontiguousarray(v) for k, v in arrays.items()}
    nc = _bacc.Bacc("TRN2", target_bir_lowering=False, num_devices=1)
    args = [nc.dram_tensor(k, v.shape, mybir.dt.from_np(v.dtype), kind="ExternalInput").ap() for k, v in arrays.items()]
    args.append(nc.dram_tensor("out_0_dram", (N, F), F32, kind="ExternalOutput").ap())
    build(nc, *args)
    r = _run(nc, [arrays], core_ids=[0])
    return r.results[0]["out_0_dram"]
```
